# Optimizing a Trainium2 kernel written in Bass

```python
import numpy as np
import jax
import jax.numpy as jnp

def _softmax(x, axis=-1):
    return jax.nn.softmax(x, axis=axis)

def _gelu(x):
    return jax.nn.gelu(x, approximate=True)

def _silu(x):
    return jax.nn.silu(x)

def _sigmoid(x):
    return jax.nn.sigmoid(x)

def _layernorm(x, axis=-1, eps=1e-05):
    m = jnp.mean(x, axis=axis, keepdims=True)
    v = jnp.var(x, axis=axis, keepdims=True)
    return (x - m) / jnp.sqrt(v + eps)

def _scatter_add(tgt, idx, src, axis=0):
    return tgt.at[idx].add(src)

def _segment_sum(src, seg, n):
    return jax.ops.segment_sum(src, seg, n)
kernel_name = 'mk_seq_postln_d1_jaxref_r8_39df27'

def setup_inputs(seed: int=0):
    np.random.seed(seed)
    _w = jnp.asarray

    def _L0_attn_setup():
        import jax, jax.numpy as jnp
        import numpy as np
        D_MODEL = 128
        NUM_HEADS = 16
        D_K = D_MODEL // NUM_HEADS
        ROPE_THETA = 10000.0

        def _apply_rope(t):
            S, dk = (t.shape[-2], t.shape[-1])
            inv_freq = 1.0 / ROPE_THETA ** (jnp.arange(0, dk, 2) / dk)
            angles = jnp.outer(jnp.arange(S), inv_freq)
            cos = jnp.repeat(jnp.cos(angles), 2, axis=-1).astype(t.dtype)
            sin = jnp.repeat(jnp.sin(angles), 2, axis=-1).astype(t.dtype)
            t_even = t[..., 0::2]
            t_odd = t[..., 1::2]
            t_rot = jnp.stack([-t_odd, t_even], axis=-1).reshape(t.shape)
            return t * cos + t_rot * sin
        key = jax.random.key(seed)
        kx, kq, kk, kv, ko = jax.random.split(key, 5)
        B, S = (4, 256)
        std = (2.0 / (D_MODEL + D_MODEL)) ** 0.5

        def w(k):
            return jax.random.truncated_normal(k, -3.0, 3.0, (D_MODEL, D_MODEL), jnp.float32) * std
        return {'x': jax.random.normal(kx, (B, S, D_MODEL), jnp.float32), 'Wq': w(kq), 'Wk': w(kk), 'Wv': w(kv), 'Wo': w(ko)}
    _L0_attn_in = _L0_attn_setup()

    def _L0_ffn_setup():
        import jax, jax.numpy as jnp
        import numpy as np
        B, S, H, E, F = (2, 256, 128, 8, 512)
        key = jax.random.key(seed)
        k1, k2, k3, k4 = jax.random.split(key, 4)
        h = jax.random.normal(k1, (B, S, H), dtype=jnp.float32)
        Wr = jax.random.normal(k2, (H, E), dtype=jnp.float32) / np.sqrt(H)
        W1 = jax.random.normal(k3, (E, H, F), dtype=jnp.float32) / np.sqrt(H)
        W2 = jax.random.normal(k4, (E, F, H), dtype=jnp.float32) / np.sqrt(F)
        return {'h': h, 'Wr': Wr, 'W1': W1, 'W2': W2}
    _L0_ffn_in = _L0_ffn_setup()
    _d = {'L0_attn_x': _L0_attn_in['x'], 'L0_attn_Wq': _L0_attn_in['Wq'], 'L0_attn_Wk': _L0_attn_in['Wk'], 'L0_attn_Wv': _L0_attn_in['Wv'], 'L0_attn_Wo': _L0_attn_in['Wo'], 'L0_ffn_Wr': _L0_ffn_in['Wr'], 'L0_ffn_W1': _L0_ffn_in['W1'], 'L0_ffn_W2': _L0_ffn_in['W2']}
    _x0 = _d['L0_attn_x']
    _d['L0_attn_x'] = jax.random.normal(jax.random.fold_in(jax.random.key(seed), 1), (4, 1024, 128), dtype=_x0.dtype)
    del _x0
    return _d

def reference(L0_attn_x, L0_attn_Wq, L0_attn_Wk, L0_attn_Wv, L0_attn_Wo, L0_ffn_Wr, L0_ffn_W1, L0_ffn_W2):

    def _L0_attn_ref(x, Wq, Wk, Wv, Wo):
        import jax, jax.numpy as jnp
        import numpy as np
        D_MODEL = 128
        NUM_HEADS = 16
        D_K = D_MODEL // NUM_HEADS
        ROPE_THETA = 10000.0

        def _apply_rope(t):
            S, dk = (t.shape[-2], t.shape[-1])
            inv_freq = 1.0 / ROPE_THETA ** (jnp.arange(0, dk, 2) / dk)
            angles = jnp.outer(jnp.arange(S), inv_freq)
            cos = jnp.repeat(jnp.cos(angles), 2, axis=-1).astype(t.dtype)
            sin = jnp.repeat(jnp.sin(angles), 2, axis=-1).astype(t.dtype)
            t_even = t[..., 0::2]
            t_odd = t[..., 1::2]
            t_rot = jnp.stack([-t_odd, t_even], axis=-1).reshape(t.shape)
            return t * cos + t_rot * sin
        B, S, D = x.shape
        H, dk = (NUM_HEADS, D_K)
        q = jnp.einsum('bsi,io->bso', x, Wq).reshape(B, S, H, dk).swapaxes(1, 2)
        k = jnp.einsum('bsi,io->bso', x, Wk).reshape(B, S, H, dk).swapaxes(1, 2)
        v = jnp.einsum('bsi,io->bso', x, Wv).reshape(B, S, H, dk).swapaxes(1, 2)
        q = _apply_rope(q)
        k = _apply_rope(k)
        scores = jnp.einsum('bhqd,bhkd->bhqk', q, k) / dk ** 0.5
        causal = jnp.tril(jnp.ones((S, S), dtype=bool))
        scores = jnp.where(causal, scores, -jnp.inf)
        attn = jax.nn.softmax(scores, axis=-1)
        out = jnp.einsum('bhqk,bhkd->bhqd', attn, v)
        out = out.swapaxes(1, 2).reshape(B, S, D)
        return jnp.einsum('bsi,io->bso', out, Wo)

    def _L0_ffn_ref(h, Wr, W1, W2):
        import jax, jax.numpy as jnp
        import numpy as np
        B, S, H, E, F = (2, 256, 128, 8, 512)
        g = jax.nn.softmax(h @ Wr, axis=-1)
        top2_w, top2_idx = jax.lax.top_k(g, 2)
        top2_w = top2_w / jnp.sum(top2_w, axis=-1, keepdims=True)
        hid = jax.nn.relu(jnp.einsum('bsh,ehf->bsef', h, W1))
        expert_out = jnp.einsum('bsef,efh->bseh', hid, W2)
        top2_out = jnp.take_along_axis(expert_out, top2_idx[..., None], axis=2)
        return jnp.sum(top2_out * top2_w[..., None], axis=2)
    x = L0_attn_x
    x = _layernorm(x + _L0_attn_ref(x, L0_attn_Wq, L0_attn_Wk, L0_attn_Wv, L0_attn_Wo), axis=-1)
    x = _layernorm(x + _L0_ffn_ref(x, L0_ffn_Wr, L0_ffn_W1, L0_ffn_W2), axis=-1)
    return x

_drawn_inputs = setup_inputs


def setup_inputs(seed=0):
    import zlib

    import numpy as np

    out = dict(_drawn_inputs(seed))
    spreads = {}
    factors = {}
    for name, (base, spread) in spreads.items():
        noise = np.random.default_rng([zlib.crc32(name.encode()), seed]).standard_normal(out[name].shape)
        drawn = base * np.exp(spread * noise) if base else spread * noise
        out[name] = jnp.asarray(drawn.astype(out[name].dtype))
    for name, factor in factors.items():
        out[name] = (out[name] * factor).astype(out[name].dtype)
    return out
```

```python
from contextlib import ExitStack

import numpy as np

import concourse.bass as bass
from concourse import mybir

F32 = mybir.dt.float32
BF16 = mybir.dt.bfloat16
U32 = mybir.dt.uint32
ALU = mybir.AluOpType
ACT = mybir.ActivationFunctionType
AX = mybir.AxisListType

P = 128
D = 128
H = 16
DK = D // H
G = 4
NG = H // G
NEG = -3.0e38
EPS = 1e-5
SHIFT_AT = 96
SLOTS = 3
RING = 4


def score_items():
    out = []
    for half in range(2):
        for j in range(4 * half + 4):
            w = 512 - max(0, P * j - 512 * half)
            out += [(half, j, (0, 1, 2, 3))] if w <= 256 else [(half, j, (0, 1)), (half, j, (2, 3))]
    return out


def max_items():
    out = []
    for i in range(8):
        if i < 2:
            out.append((0, i, (0, 1, 2, 3)))
        elif i < 4:
            out += [(0, i, (0, 1)), (0, i, (2, 3))]
        else:
            out += [(1, i, (h,)) for h in range(G)]
    return out


E_ITEMS = score_items()
M_ITEMS = max_items()
NE, NM = len(E_ITEMS), len(M_ITEMS)
M_HALF = sum(1 for m in M_ITEMS if m[0] == 0)
E_HALF = sum(1 for e in E_ITEMS if e[0] == 0)
DIAGONAL = [j >= 4 * half for half, j, _ in E_ITEMS]
PV_GROUPS = sorted({(half, j) for half, j, _ in E_ITEMS})
PV_LAST = [max(n for n, e in enumerate(E_ITEMS) if e[:2] == g) for g in PV_GROUPS]
GROUP_OF = [PV_GROUPS.index(e[:2]) for e in E_ITEMS]
NPV = len(PV_GROUPS)


def numbered(steps):
    out, n = [], 0
    for step in steps:
        out.append((*step, n))
        n += step[0] not in "CL"
    return out, n


def steps_of_batch(last):
    steps = []
    for g in range(NG):
        maxima = not (last and g == NG - 1)
        proj = {} if last else {0: {6: 0, 12: 1, 17: 2}, 1: {6: 3, 12: 4, 17: 5}}.get(g, {})
        m = 0
        for e in range(NE):
            until = (M_HALF * (e + 1) // E_HALF if e < E_HALF
                     else M_HALF + (NM - M_HALF) * (e + 1 - E_HALF) // (NE - E_HALF))
            while maxima and m < until:
                steps.append(("M", g, m))
                m += 1
                if m in (M_HALF, NM):
                    steps.append(("MT", g, int(m == NM)))
            steps.append(("E", g, e))
            if e == 2 and g > 0:
                steps.append(("C", g - 1, 1))
            if e == 4 and g > 0:
                steps.append(("N", g - 1, 1))
            if e == 8:
                steps.append(("C", g, 0))
            if e == 10:
                steps.append(("N", g, 0))
            if e in proj:
                steps.append(("P", g, proj[e]))
    steps += [("C", NG - 1, 1), ("N", NG - 1, 1), ("AT", 0, 0), ("O", 0, 0), ("L", 0, 0),
              ("XT", 0, 0), ("LG", 0, 0), ("CT", 0, 0)]
    return numbered(steps)


def steps_before():
    steps = [("P", 0, n) for n in range(6)]
    for m in range(NM):
        steps.append(("M", -1, m))
        if m + 1 in (M_HALF, NM):
            steps.append(("MT", -1, int(m + 1 == NM)))
    return numbered(steps)


def build(nc, x, Wq, Wk, Wv, Wo, Wr, W1, W2, cos, sin, out):
    B, S, _ = x.shape
    E, _, F = W1.shape
    NT = S // P
    FC = F // P
    T = B * NT
    NTILES = 2 * T + E
    REGION = (T + 1) * P
    RT, RT_CNT = 38, 17
    SCALE = float(DK) ** -0.5
    assert S == 1024 and D == P and F == 512 and E == 8

    before, n_before = steps_before()
    body, n_body = steps_of_batch(False)
    tail, _ = steps_of_batch(True)
    assert n_before % SLOTS == 0 and n_body % SLOTS == 0

    ctx = ExitStack()
    with ctx:
        def sb(name, shape, dt=F32):
            return ctx.enter_context(nc.sbuf_tensor(name, shape, dt))

        def sem(name):
            return ctx.enter_context(nc.semaphore(name))

        slot = [ctx.enter_context(nc.psum_tensor(f"slot{i}", [P, 2, 512], F32)) for i in range(SLOTS)]
        opsum = [ctx.enter_context(nc.psum_tensor(f"opsum{i}", [P, 512], F32)) for i in range(2)]

        ident = sb("ident", [P, P])
        identb = sb("identb", [P, P], BF16)
        maskb = sb("maskb", [P, P], BF16)
        before_b = sb("before_b", [P, P], BF16)
        onesb = sb("onesb", [P, P], BF16)
        neg_half = sb("neg_half", [P, NT])
        zeros = sb("zeros", [P, D])
        counts = sb("counts", [P, NTILES], mybir.dt.int32)
        first_rows = sb("first_rows", [P, E])
        rev = sb("rev", [P, E])
        tile_no = sb("tile_no", [P, NTILES])
        xall = sb("xall", [P, T, D])
        w1s = sb("w1s", [P, E, F])
        wr = sb("wr", [P, E])
        chosen = sb("chosen", [P, 2, T, E])
        gates = sb("gates", [P, 2, T])
        row_f = sb("row_f", [P, 2, T])
        x_row = sb("x_row", [P, 2, T], U32)
        y_row = sb("y_row", [P, 2, T], U32)
        run = sb("run", [P, NT + 1, E])
        stat = sb("stat", [P, 4, NT])
        tinfo = sb("tinfo", [P, 3, NTILES], mybir.dt.int32)
        x_rows = nc.dram_tensor("x_rows", ((E + 1) * REGION, D), F32).ap()
        y_rows = nc.dram_tensor("y_rows", (NTILES * P, D), F32).ap()

        attention = ctx.enter_context(ExitStack())

        def sb(name, shape, dt=F32):
            return attention.enter_context(nc.sbuf_tensor(name, shape, dt))

        wq, wk, wv, wo = (sb(n, [P, D]) for n in ("wq", "wk", "wv", "wo"))
        wqr, wkr = sb("wqr", [P, D]), sb("wkr", [P, D])
        cosT, sinT = sb("cosT", [P, S]), sb("sinT", [P, S])
        xT = sb("xT", [P, S])
        tcos, tsin = sb("tcos", [P, S]), sb("tsin", [P, S])
        rope = sb("rope", [P, S])
        rest = sb("rest", [P, S])
        parts = sb("parts", [P, 2, 3, S], BF16)
        vraw = sb("vraw", [P, NT, D])
        vaug = [sb(f"vaug{g}", [P, NT, G, 32]) for g in range(NG)]
        stq = [sb(f"stq{g}", [P, 2, G, 512], BF16) for g in range(NG)]
        stk = [sb(f"stk{g}", [P, G, S], BF16) for g in range(NG)]
        negm = sb("negm", [P, 2, 2, 16])
        mrow = sb("mrow", [16, 2, P])
        mrest = sb("mrest", [16, 2, P])
        mparts = sb("mparts", [16, 2, 3, P], BF16)
        probs = [sb(f"probs{i}", [P, 2, 512]) for i in range(RING)]
        osb = sb("osb", [P, 2, 512])
        rsum = sb("rsum", [P, 2, 4, G])
        attn = sb("attn", [P, NT, D])
        attnT = tcos
        res = rest[:, :].rearrange("p (t d) -> p t d", t=NT)
        sq = rope[:, :].rearrange("p (t d) -> p t d", t=NT)
        rt = [sb(f"rt{i}", [P, NT, E]) for i in range(5)]
        cntb = sb("cntb", [P, NT, E], BF16)
        rs = sb("rs", [P, 4, NT])
        tbl = sb("tbl", [P, 8, NTILES])
        x1 = sb("x1", [P, NT, D])
        xr = sb("xr", [P, 2, NT], U32)
        xnext = sb("xnext", [P, NT, D])

        q_dram = nc.dram_tensor("q_dram", (B, H, 3, DK, S), BF16).ap()
        k_dram = nc.dram_tensor("k_dram", (B, H, 5, DK, S), BF16).ap()

        x_in = sem("x_in")
        w_in = sem("w_in")
        consts = sem("consts")
        wrot = sem("wrot")
        filled = [sem(f"filled{i}") for i in range(SLOTS)]
        left = [sem(f"left{i}") for i in range(SLOTS)]
        vaug_done = sem("vaug_done")
        pool_chain = sem("pool_chain")
        parts_done = sem("parts_done")
        parts_out = sem("parts_out")
        stack_in = [sem(f"stack_in{g}") for g in range(NG)]
        mparts_done = sem("mparts_done")
        mrow_in = [sem(f"mrow_in{i}") for i in range(2)]
        masked = sem("masked")
        pv_done = sem("pv_done")
        osb_done = sem("osb_done")
        dve_chain = sem("dve_chain")
        dve_recip = sem("dve_recip")
        max_chain = sem("max_chain")
        pool_settled = sem("pool_settled")
        dve_settled = sem("dve_settled")
        xnow_done = sem("xnow_done")
        xnext_done = sem("xnext_done")
        ln_sq = sem("ln_sq")
        ln_var = sem("ln_var")
        ln_pow = sem("ln_pow")
        x1_kept = sem("x1_kept")
        x1_free = sem("x1_free")
        run_zero = sem("run_zero")
        x1_done = sem("x1_done")
        wr_in = sem("wr_in")
        we_in = sem("we_in")
        spare_in = sem("spare_in")
        rt_chain = sem("rt_chain")
        rt_exp = sem("rt_exp")
        rows_done = sem("rows_done")
        scattered = sem("scattered")
        table_done = sem("table_done")
        out_done = sem("out_done")
        N_CONSTS = 15 + 5 * NG

        phase = ctx.enter_context(ExitStack())
        block = phase.enter_context(nc.Block())

        def every_batch(eng, do):
            with eng.Fori(0, B - 1) as b:
                do(b, body, False)
            do(B - 1, tail, True)

        def slot_of(b, n):
            return n % SLOTS, (n // SLOTS if b is None else (n_before + b * n_body + n - n % SLOTS) // SLOTS
                               if isinstance(b, int) else n_before // SLOTS + n // SLOTS + b * (n_body // SLOTS))

        def taken(eng, b, steps, kind, g, m):
            n = next(x[3] for x in steps if x[:3] == (kind, g, m))
            s, used = slot_of(b, n)
            eng.wait_ge(left[s], used + 1)

        def place(heads, h, w):
            return h % 2, (h // 2) * w if len(heads) == G else 0

        def width(half, j):
            return 512 - max(0, P * j - 512 * half)

        def tokens(b):
            return slice(NT * b, NT * b + NT) if isinstance(b, int) else bass.ds(b * NT, NT)

        def bc(s_):
            return s_.unsqueeze(2).to_broadcast([P, s_.shape[1], D])

        def norm_squares(pool, k, y, sq):
            pool.wait_ge(dve_chain, 4 * k + 3)
            nc.gpsimd.tensor_tensor(sq, y, y, ALU.mult).then_inc(ln_sq, 1)
            pool.wait_ge(ln_var, k + 1)
            nc.gpsimd.tensor_tensor(stat[:, 3, :], stat[:, 0, :], neg_half[:, :], ALU.pow).then_inc(ln_pow, 1)

        def layer_norm_on(dve, sq):
            def norm(k, y):
                def link(i, ins):
                    ins.then_inc(dve_chain, 1)
                    dve.wait_ge(dve_chain, 4 * k + i)
                v = nc.vector
                link(1, v.tensor_reduce(stat[:, 0, :], y, AX.X, ALU.add))
                link(2, v.tensor_scalar(stat[:, 1, :], stat[:, 0, :], 1.0 / D, None, ALU.mult))
                link(3, v.tensor_tensor(y, y, bc(stat[:, 1, :]), ALU.subtract))
                dve.wait_ge(ln_sq, k + 1)
                link(4, v.tensor_reduce(stat[:, 2, :], sq, AX.X, ALU.add))
                v.tensor_scalar(stat[:, 0, :], stat[:, 2, :], 1.0 / D, EPS, ALU.mult, ALU.add).then_inc(ln_var, 1)
                dve.wait_ge(ln_pow, k + 1)
            return norm

        @block.sync
        def _(sp):
            xv = x.rearrange("b (t p) d -> p (b t) d", p=P)
            for b in range(B):
                sp.dma_start(xall[:, b * NT:(b + 1) * NT, :], xv[:, b * NT:(b + 1) * NT, :]).then_inc(x_in, 16)
                if b == 0:
                    for dst, src in ((wq, Wq), (wk, Wk), (wv, Wv), (wo, Wo), (cosT, cos), (sinT, sin)):
                        sp.dma_start(dst[:, :], src).then_inc(w_in, 16)

            sp.dma_start(wr[:, :], Wr).then_inc(wr_in, 16)
            sp.dma_start(w1s[:, :, :], W1.rearrange("e h f -> h e f")).then_inc(we_in, 16)

            def store_parts(bb, which):
                sp.wait_ge(parts_done, 2 * bb + which + 1)
                dram = (q_dram, k_dram)[which]
                for at in range(dram.shape[2]):
                    sp.dma_start(dram[bb, :, at], parts[:, which, at % 3, :]).then_inc(parts_out, 16)

            def load_stack(bb, g):
                sp.wait_ge(parts_out, 128 * bb + 128)
                heads = slice(G * g, G * g + G)
                for r in range(3):
                    rows = slice(3 * DK * r, 3 * DK * (r + 1))
                    q_src = q_dram[bb, heads].rearrange("h n d s -> (n d) h s")
                    for half in range(2):
                        sp.dma_start(stq[g][rows, half, :, :],
                                     q_src[:, :, 512 * half:512 * half + 512]).then_inc(stack_in[g], 16)
                    sp.dma_start(stk[g][rows, :, :],
                                 k_dram[bb, heads, r:r + 3].rearrange("h n d s -> (n d) h s")).then_inc(stack_in[g], 16)

            def shift_rows(u, g, half):
                sp.wait_ge(mparts_done, 2 * u + half + 1)
                for part in range(3):
                    sp.dma_start(stq[g][SHIFT_AT + part:SHIFT_AT + part + 1, half, :, :],
                                 mparts[:, half, part, :]).then_inc(mrow_in[half], 16)

            store_parts(0, 0)
            store_parts(0, 1)
            sp.wait_ge(consts, N_CONSTS)
            for t in range(NTILES - 2 * T):
                sp.dma_start(x_rows[E * REGION + P * t:E * REGION + P * (t + 1), :], zeros[:, :]).then_inc(spare_in, 16)
            for g in range(NG):
                load_stack(0, g)
            for half in range(2):
                shift_rows(0, 0, half)

            def batch(b, steps, last):
                for kind, g, m, n in steps:
                    if kind == "MT":
                        shift_rows(NG * b + g + 1, (g + 1) % NG, m)
                    if last or kind != "E":
                        continue
                    if (g, m) == (1, 13):
                        store_parts(b + 1, 0)
                    if (g, m) == (2, 13):
                        store_parts(b + 1, 1)
                        taken(sp, b, steps, "E", 0, NE - 1)
                        load_stack(b + 1, 0)
                    if (g, m) == (3, 6):
                        taken(sp, b, steps, "E", 1, NE - 1)
                        load_stack(b + 1, 1)
                if not last:
                    for g in (2, 3):
                        taken(sp, b, steps, "E", g, NE - 1)
                        load_stack(b + 1, g)

            every_batch(sp, batch)
        @block.tensor
        def _(pe):
            pe.sem_inc(pv_done, 1)
            pe.wait_ge(consts, N_CONSTS)
            pe.wait_ge(x_in, 16 * B)
            pe.wait_ge(w_in, 96)

            def pv_group(b, steps, g, n):
                half, j = PV_GROUPS[n]
                u = NG * b + g
                taken(pe, b, steps, "E", g, PV_LAST[n])
                if DIAGONAL[PV_LAST[n]]:
                    pe.wait_ge(masked, sum(DIAGONAL) * u + sum(DIAGONAL[:PV_LAST[n] + 1]))
                if j == 0:
                    if half == 0:
                        pe.wait_ge(vaug_done, u + 1)
                    pe.wait_ge(osb_done, 2 * u + 1 + half)
                w = width(half, j)
                for h in range(G):
                    k = next(k for k in range(NE) if GROUP_OF[k] == n and h in E_ITEMS[k][2])
                    bank, col = place(E_ITEMS[k][2], h, w)
                    mm = nc.tensor.matmul(opsum[half][32 * h:32 * h + 32, 512 - w:512], vaug[g][:, j, h, :],
                                          probs[k % RING][:, bank, col:col + w],
                                          start=(j == 0), stop=(j == 4 * half + 3), skip_group_check=True)
                mm.then_inc(pv_done, 1)

            def fill(b, steps, kind, g, m, n):
                s, used = slot_of(b, n)
                ps = slot[s]
                if not (b is None and n < SLOTS):
                    pe.wait_ge(left[s], used)
                at = lambda t: ps[:, t // 4, P * (t % 4):P * (t % 4) + P]
                if kind == "P" and m == 0:
                    for t in range(NT):
                        src = xall[:, t, :] if b is None else xnext[:, t, :]
                        if b is not None and t == 0:
                            pe.wait_ge(xnext_done, b + 1)
                        mm = nc.tensor.transpose(at(t), src, ident[:, :])
                elif kind == "P":
                    if m == 1:
                        taken(pe, b, steps, "P", 0, 0)
                        pe.wait_ge(wrot, 4)
                    if m < 5:
                        w = (wq, wqr, wk, wkr)[m - 1]
                        for c in range(2):
                            mm = nc.tensor.matmul(ps[:, c, :], w[:, :], xT[:, 512 * c:512 * c + 512],
                                                  start=True, stop=True)
                    else:
                        for t in range(NT):
                            mm = nc.tensor.matmul(at(t), xT[:, P * t:P * t + P], wv[:, :], start=True, stop=True,
                                                  skip_group_check=True)
                elif kind == "M":
                    half, i, heads = M_ITEMS[m]
                    ug = (g + 1) % NG
                    if m == 0:
                        bb = 0 if b is None else b + (g + 1) // NG
                        pe.wait_ge(stack_in[ug], 16 * 9 * (bb + 1))
                    keys = P * (i + 1)
                    for h in heads:
                        for c in range(0, keys, 512):
                            w = min(512, keys - c)
                            bank, col = (c // 512, 0) if len(heads) == 1 else place(heads, h, keys)
                            diag = c + w == keys
                            mm = nc.tensor.matmul(ps[:, bank, col:col + w], stq[ug][0:SHIFT_AT, half, h, P * (i % 4):P * (i % 4) + P],
                                                  stk[ug][0:SHIFT_AT, h, c:c + w], start=True, stop=not diag,
                                                  skip_group_check=True)
                            if diag:
                                mm = nc.tensor.matmul(ps[:, bank, col + w - P:col + w], identb[:, :], maskb[:, :],
                                                      start=False, stop=True, skip_group_check=True)
                elif kind == "MT":
                    taken(pe, b, steps, "M", g, NM - 1 if m else M_HALF - 1)
                    mm = nc.tensor.transpose(ps[0:16, 0, 0:P], negm[:, (g + 1) % 2, m, :], ident[:, :])
                elif kind == "E":
                    half, j, heads = E_ITEMS[m]
                    if m in (0, E_HALF):
                        pe.wait_ge(mrow_in[half], 48 * (NG * b + g + 1))
                    w = width(half, j)
                    for h in heads:
                        bank, col = place(heads, h, w)
                        mm = nc.tensor.matmul(ps[:, bank, col:col + w], stk[g][:, h, P * j:P * j + P],
                                              stq[g][:, half, h, 512 - w:512],
                                              start=True, stop=True, skip_group_check=True)
                elif kind == "N":
                    pe.wait_ge(osb_done, 2 + 2 * (NG * b + g) + m + 1)
                    for t in range(4):
                        mm = nc.tensor.transpose(ps[:, 0, P * t:P * t + P], osb[:, m, P * t:P * t + P], ident[:, :])
                elif kind == "AT":
                    taken(pe, b, steps, "N", NG - 1, 1)
                    for t in range(NT):
                        mm = nc.tensor.transpose(at(t), attn[:, t, :], ident[:, :])
                elif kind == "XT":
                    pe.wait_ge(x1_done, b + 1)
                    for t in range(NT):
                        mm = nc.tensor.transpose(at(t), x1[:, t, :], ident[:, :])
                elif kind == "LG":
                    taken(pe, b, steps, "XT", 0, 0)
                    pe.wait_ge(wr_in, 16)
                    for t in range(NT):
                        mm = nc.tensor.matmul(ps[:, 0, E * t:E * t + E], attnT[:, P * t:P * t + P], wr[:, :],
                                              start=True, stop=True, skip_group_check=True)
                elif kind == "CT":
                    pe.wait_ge(rt_chain, RT * b + RT_CNT)
                    for c, w in enumerate((before_b, onesb)):
                        mm = nc.tensor.matmul(ps[:, 0, NT * E * c:NT * E * (c + 1)], w[:, :],
                                              cntb[:, :, :].rearrange("p t e -> p (t e)"), start=True, stop=True,
                                              skip_group_check=True)
                elif kind == "O":
                    taken(pe, b, steps, "AT", 0, 0)
                    for t in range(NT):
                        mm = nc.tensor.matmul(at(t), attnT[:, P * t:P * t + P], wo[:, :], start=True, stop=True,
                                              skip_group_check=True)
                mm.then_inc(filled[s], 1)

            for kind, g, m, n in before:
                fill(None, before, kind, g, m, n)

            def batch(b, steps, last):
                waiting = []
                for kind, g, m, n in steps:
                    if kind == "C":
                        while waiting and waiting[0] <= (g, NPV - 1 if m else 3):
                            pv_group(b, steps, *waiting.pop(0))
                    if kind in "CL":
                        continue
                    fill(b, steps, kind, g, m, n)
                    if kind == "E":
                        while waiting and NE * waiting[0][0] + PV_LAST[waiting[0][1]] <= NE * g + m - 2:
                            pv_group(b, steps, *waiting.pop(0))
                        if m in PV_LAST:
                            waiting.append((g, PV_LAST.index(m)))

            every_batch(pe, batch)

        @block.scalar
        def _(act):
            act.sem_inc(osb_done, 2)

            def batch(b, steps, last):
                for kind, g, m, n in steps:
                    s, used = slot_of(b, n)
                    flat = slot[s][:, :, :].rearrange("p a c -> p (a c)")
                    if kind == "P" and m == 0:
                        act.wait_ge(filled[s], used + 1)
                        nc.scalar.activation(xT[:, :], flat, ACT.Copy).then_inc(left[s], 1)
                    if kind == "P" and m == 5:
                        act.wait_ge(filled[s], used + 1)
                        if b is not None:
                            act.wait_ge(vaug_done, NG * (b + 1))
                        nc.scalar.activation(vraw[:, :, :].rearrange("p a c -> p (a c)"), flat,
                                             ACT.Copy).then_inc(left[s], 1)
                    if kind == "E":
                        half, j, heads = E_ITEMS[m]
                        e = NE * g + m - RING
                        act.wait_ge(pv_done, 1 + NPV * NG * b + (NPV * (e // NE) + GROUP_OF[e % NE] + 1 if e >= 0 else 0))
                        act.wait_ge(filled[s], used + 1)
                        wide = width(half, j) * len(heads) // 2
                        nc.scalar.activation(probs[m % RING][:, :, 0:wide], slot[s][:, :, 0:wide], ACT.Exp,
                                             scale=SCALE).then_inc(left[s], 1)
                    if kind == "C":
                        act.wait_ge(pv_done, 1 + NPV * (NG * b + g) + (NPV if m else 4))
                        nc.scalar.activation(osb[:, m, :], opsum[m][:, :], ACT.Copy).then_inc(osb_done, 1)
                    if kind == "LG":
                        act.wait_ge(rt_chain, RT * b + 2)
                        nc.scalar.activation(rt[1][:, :, :], rt[0][:, :, :], ACT.Exp).then_inc(rt_exp, 1)
                    if kind in ("AT", "XT"):
                        act.wait_ge(filled[s], used + 1)
                        nc.scalar.activation(attnT[:, :], flat, ACT.Copy).then_inc(left[s], 1)

            batch(None, before, False)
            every_batch(act, batch)

        @block.vector
        def _(dve):
            links = [0]

            dve.wait_ge(consts, 15 + 3 * NG)
            for g in range(NG):
                nc.vector.memset(stk[g][SHIFT_AT:SHIFT_AT + 3, :, :], 1.0).then_inc(consts, 1)
            dve.wait_ge(w_in, 96)
            for w, r in ((wq, wqr), (wk, wkr)):
                pair = w[:, :].rearrange("p (c two) -> p c two", two=2)
                rot = r[:, :].rearrange("p (c two) -> p c two", two=2)
                nc.vector.tensor_scalar(rot[:, :, 0], pair[:, :, 1], -1.0, None, ALU.mult).then_inc(wrot, 1)
                nc.vector.tensor_copy(rot[:, :, 1], pair[:, :, 0]).then_inc(wrot, 1)

            def batch(b, steps, last):
                for kind, g, m, n in steps:
                    s, used = slot_of(b, n)
                    ps = slot[s]
                    flat = ps[:, :, :].rearrange("p a c -> p (a c)")
                    if kind == "P" and 1 <= m < 5:
                        bb = 0 if b is None else b + 1
                        dve.wait_ge(filled[s], used + 1)
                        if m in (1, 3) and not (b is None and m == 1):
                            dve.wait_ge(parts_done, 2 * bb + (m == 3))
                        if m % 2:
                            nc.vector.tensor_tensor(tcos[:, :], flat, cosT[:, :], ALU.mult).then_inc(left[s], 1)
                        else:
                            nc.vector.tensor_tensor(tsin[:, :], flat, sinT[:, :], ALU.mult).then_inc(left[s], 1)
                        if b is not None and m == 4:
                            pass
                    if kind == "M":
                        half, i, heads = M_ITEMS[m]
                        dve.wait_ge(filled[s], used + 1)
                        keys = P * (i + 1)
                        out_ = negm[:, (g + 1) % 2, half, :].rearrange("p (j a q) -> p a j q", a=2, j=2)
                        q = i % 4
                        if len(heads) == G:
                            src = ps[:, :, 0:2 * keys].rearrange("p a (j k) -> p a j k", j=2)
                            dst = out_[:, :, :, q]
                        elif len(heads) == 2:
                            src = ps[:, :, 0:keys]
                            dst = out_[:, :, heads[0] // 2, q]
                        else:
                            src = flat[:, 0:keys]
                            dst = out_[:, heads[0] % 2, heads[0] // 2, q:q + 1]
                        nc.vector.tensor_reduce(dst, src, AX.X, ALU.max, negate=True).then_inc(left[s], 1)
                    if kind == "MT":
                        u = 0 if b is None else NG * b + g + 1
                        dve.wait_ge(filled[s], used + 1)
                        if b is not None:
                            dve.wait_ge(mparts_done, 2 * (u - 1) + m + 1)
                        nc.vector.tensor_copy(mrow[:, m, :], ps[0:16, 0, 0:P]).then_inc(left[s], 1)
                    if kind == "N":
                        u = NG * b + g
                        dve.wait_ge(filled[s], used + 1)
                        view = ps[:, 0, :].rearrange("p (t h c) -> p t h c", t=4, h=G)
                        nc.vector.reciprocal(rsum[:, m, :, :], view[:, :, :, DK]).then_inc(dve_recip, 1)
                        dve.wait_ge(dve_recip, 2 * u + m + 1)
                        nc.vector.tensor_tensor(
                            attn[:, 4 * m:4 * m + 4, G * DK * g:G * DK * (g + 1)].rearrange("p t (h c) -> p t h c", h=G),
                            view[:, :, :, 0:DK], rsum[:, m, :, :].unsqueeze(3).to_broadcast([P, 4, G, DK]),
                            ALU.mult).then_inc(left[s], 1)
                    if kind == "O":
                        dve.wait_ge(filled[s], used + 1)
                        nc.vector.tensor_tensor(res, ps[:, :, :].rearrange("p a (c d) -> p (a c) d", d=D),
                                                xall[:, tokens(b), :], ALU.add).then_inc(left[s], 1)
                    if kind == "L":
                        so, uo = slot_of(b, n - 1)
                        dve.wait_ge(left[so], uo + 1)
                        layer_norm(b, res)
                        dve.wait_ge(x1_free, b + 1)
                        nc.vector.tensor_tensor(x1[:, :, :], res, bc(stat[:, 3, :]), ALU.mult).then_inc(x1_done, 1)
                        dve.wait_ge(x1_done, b + 1)
                        settled()
                        nc.vector.tensor_copy(xall[:, tokens(b), :], x1[:, :, :]).then_inc(x1_kept, 1)
                    if kind == "LG":
                        dve.wait_ge(filled[s], used + 1)
                        choose(b, ps[:, 0, 0:NT * E].rearrange("p (t e) -> p t e", e=E), left[s], used)
                    if kind == "CT":
                        dve.wait_ge(filled[s], used + 1)
                        rank(b, ps[:, 0, 0:2 * NT * E].rearrange("p (w t e) -> p w t e", w=2, e=E), left[s], used)
                    if kind == "P" and m == 4 and b is not None:
                        pass
                    if kind == "E" and (g, m) == (0, 2) and not last:
                        nc.vector.tensor_copy(xnext[:, :, :], xall[:, tokens(b + 1), :]).then_inc(xnext_done, 1)

            def tables(dve):
                v = nc.vector
                done = [0]

                def step(ins):
                    done[0] += 1
                    ins.then_inc(table_done, 1)
                    dve.wait_ge(table_done, done[0])
                n_e = run[:, 0, :]
                share = tbl[:, 0, 0:E]
                n_tiles = tbl[:, 1, 0:E]
                end = tbl[:, 2, 0:E + 1]
                shift = tbl[:, 3, 0:E]
                is_over = tsin[:, 0:NTILES * E].rearrange("p (t e) -> p t e", e=E)
                over_tiles_of = sinT[:, 0:NTILES * E].rearrange("p (t e) -> p t e", e=E)
                begun = tsin[:, 0:E * T].rearrange("p (e t) -> p e t", e=E)
                mine = sinT[:, 0:T * E].rearrange("p (t e) -> p t e", e=E)
                wide = lambda s_, n: s_.unsqueeze(1).to_broadcast([P, n, s_.shape[1]])
                deep = lambda s_, n: s_.unsqueeze(2).to_broadcast([P, s_.shape[1], n])
                step(v.tensor_scalar(share, n_e, 1.0 / P, None, ALU.mult))
                step(v.tensor_tensor(begun, deep(share, T), wide(tile_no[:, 0:T], E), ALU.is_gt))
                step(v.tensor_reduce(n_tiles, begun, AX.X, ALU.add))
                step(v.memset(end[:, 0:1], 0.0))
                for e in range(E):
                    step(v.tensor_tensor(end[:, e + 1:e + 2], end[:, e:e + 1], n_tiles[:, e:e + 1], ALU.add))
                step(v.scalar_tensor_tensor(shift, end[:, 0:E], float(P), first_rows[:, :], ALU.mult, ALU.subtract))
                for k in range(2):
                    step(v.tensor_tensor(mine, chosen[:, k], wide(shift, T), ALU.mult))
                    step(v.tensor_reduce(tbl[:, 4, 0:T], mine, AX.X, ALU.add))
                    step(v.tensor_tensor(tbl[:, 5, 0:T], tbl[:, 4, 0:T], row_f[:, k, :], ALU.add))
                    step(v.tensor_copy(y_row[:, k, :], tbl[:, 5, 0:T]))
                step(v.tensor_tensor(is_over, deep(tile_no[:, :], E), wide(end[:, 1:E + 1], NTILES), ALU.is_ge))
                expert, tiles_over, row = (tbl[:, i, 0:NTILES] for i in (6, 7, 4))
                step(v.tensor_reduce(expert, is_over, AX.X, ALU.add))
                step(v.tensor_tensor(over_tiles_of, is_over, wide(n_tiles, NTILES), ALU.mult))
                step(v.tensor_reduce(tiles_over, over_tiles_of, AX.X, ALU.add))
                step(v.tensor_tensor(row, tile_no[:, :], tiles_over, ALU.subtract))
                step(v.tensor_scalar(tiles_over, expert, float(REGION), None, ALU.mult))
                step(v.scalar_tensor_tensor(row, row, float(P), tiles_over, ALU.mult, ALU.add))
                step(v.tensor_copy(tinfo[:, 1, :], row))
                step(v.tensor_scalar(expert, expert, float(E - 1), None, ALU.min))
                step(v.tensor_copy(tinfo[:, 0, :], expert))
                step(v.tensor_tensor(shift, first_rows[:, :], n_e, ALU.add))
                step(v.tensor_copy(tinfo[:, 2, 0:E], shift))

            layer_norm = layer_norm_on(dve, sq)

            def settled():
                dve.sem_inc(dve_settled, 1)

            def over_experts(s_):
                return s_.unsqueeze(2).to_broadcast([P, s_.shape[1], E])

            def over_tiles(s_):
                return s_.unsqueeze(1).to_broadcast([P, NT, E])

            def choose(b, logits, left_s, used):
                v = nc.vector

                def step(i, ins):
                    ins.then_inc(rt_chain, 1)
                    dve.wait_ge(rt_chain, RT * b + i)
                cut, ex, g, cand, tmp = (x[:, :, :] for x in rt)
                one, two = (chosen[:, k, tokens(b), :] for k in range(2))
                step(1, v.tensor_reduce(rs[:, 0, :], logits, AX.X, ALU.max))
                step(2, v.tensor_tensor(cut, logits, over_experts(rs[:, 0, :]), ALU.subtract))
                dve.wait_ge(rt_exp, b + 1)
                step(3, v.tensor_reduce(rs[:, 1, :], ex, AX.X, ALU.add))
                step(4, v.reciprocal(rs[:, 2, :], rs[:, 1, :]))
                step(5, v.tensor_tensor(g, ex, over_experts(rs[:, 2, :]), ALU.mult))
                i = 5
                for k, pick in enumerate((one, two)):
                    step(i + 1, v.tensor_reduce(rs[:, k, :], g, AX.X, ALU.max))
                    step(i + 2, v.tensor_tensor(tmp, g, over_experts(rs[:, k, :]), ALU.is_equal))
                    step(i + 3, v.tensor_tensor(cand, tmp, over_tiles(rev[:, :]), ALU.mult))
                    step(i + 4, v.tensor_reduce(rs[:, 3, :], cand, AX.X, ALU.max))
                    step(i + 5, v.tensor_tensor(tmp if k else cut, over_tiles(rev[:, :]), over_experts(rs[:, 3, :]),
                                                ALU.is_equal))
                    i += 5
                    if k == 0:
                        step(11, v.scalar_tensor_tensor(g, cut, -2.0, g, ALU.mult, ALU.add))
                        i = 11
                step(17, v.tensor_tensor(cntb[:, :, :], cut, tmp, ALU.add))
                settled()
                step(18, v.tensor_copy(one, cut))
                settled()
                step(19, v.tensor_copy(two, tmp))
                step(20, v.tensor_tensor(rs[:, 2, :], rs[:, 0, :], rs[:, 1, :], ALU.add))
                step(21, v.reciprocal(rs[:, 3, :], rs[:, 2, :]))
                gate = [gates[:, k, tokens(b)] for k in range(2)]
                step(22, v.tensor_tensor(gate[0], rs[:, 0, :], rs[:, 3, :], ALU.mult))
                v.tensor_tensor(gate[1], rs[:, 1, :], rs[:, 3, :], ALU.mult).then_inc(left_s, 1)
                dve.wait_ge(left_s, used + 1)

            def rank(b, count, left_s, used):
                v = nc.vector

                def step(i, ins):
                    ins.then_inc(rt_chain, 1)
                    dve.wait_ge(rt_chain, RT * b + 22 + i)
                cut, ex, g, cand, tmp = (x[:, :, :] for x in rt)
                for t in range(NT):
                    step(t + 1, v.tensor_tensor(run[:, t + 1, :], run[:, t, :], count[:, 1, t, :], ALU.add))
                step(9, v.tensor_tensor(g, count[:, 0], run[:, 0:NT, :], ALU.add))
                step(10, v.tensor_copy(run[:, 0, :], run[:, NT, :]))
                step(11, v.tensor_tensor(cand, g, over_tiles(first_rows[:, :]), ALU.add))
                step(12, v.tensor_tensor(ex, cand, cut, ALU.mult))
                step(13, v.tensor_tensor(g, cand, tmp, ALU.mult))
                step(14, v.tensor_reduce(row_f[:, 0, tokens(b)], ex, AX.X, ALU.add))
                step(15, v.tensor_reduce(row_f[:, 1, tokens(b)], g, AX.X, ALU.add))
                settled()
                step(16, v.tensor_copy(xr[:, :, :], row_f[:, :, tokens(b)]))
                settled()
                v.tensor_copy(rs[:, 0:2, :], row_f[:, :, tokens(b)]).then_inc(left_s, 1)
                dve.wait_ge(left_s, used + 1)

            nc.vector.memset(run[:, 0, :], 0.0).then_inc(run_zero, 1)
            dve.wait_ge(run_zero, 1)
            batch(None, before, False)
            every_batch(dve, batch)
            tables(dve)

        @block.gpsimd
        def _(pool):
            pool.sem_inc(x1_free, 1)
            nc.gpsimd.memset(ident[:, :], 0.0).then_inc(consts, 1)
            nc.gpsimd.memset(maskb[:, :], 0.0).then_inc(consts, 1)
            pool.wait_ge(consts, 2)
            nc.gpsimd.affine_select(out=ident[:, :], in_=ident[:, :], compare_op=ALU.not_equal, fill=1.0, base=0,
                                    pattern=[[-1, P]], channel_multiplier=1).then_inc(consts, 1)
            nc.gpsimd.affine_select(out=maskb[:, :], in_=maskb[:, :], compare_op=ALU.is_ge, fill=NEG, base=0,
                                    pattern=[[-1, P]], channel_multiplier=1).then_inc(consts, 1)
            pool.wait_ge(consts, 4)
            nc.gpsimd.tensor_copy(identb[:, :], ident[:, :]).then_inc(consts, 1)
            nc.gpsimd.memset(neg_half[:, :], -0.5).then_inc(consts, 1)
            nc.gpsimd.memset(zeros[:, :], 0.0).then_inc(consts, 1)
            nc.gpsimd.memset(onesb[:, :], 1.0).then_inc(consts, 1)
            nc.gpsimd.memset(before_b[:, :], 1.0).then_inc(consts, 1)
            nc.gpsimd.iota(counts[:, :], [[1, NTILES]], base=0, channel_multiplier=0).then_inc(consts, 1)
            pool.wait_ge(consts, 10)
            nc.gpsimd.affine_select(out=before_b[:, :], in_=before_b[:, :], compare_op=ALU.is_gt, fill=0.0, base=0,
                                    pattern=[[1, P]], channel_multiplier=-1).then_inc(consts, 1)
            nc.gpsimd.tensor_copy(tile_no[:, :], counts[:, :]).then_inc(consts, 1)
            pool.wait_ge(consts, 12)
            nc.gpsimd.tensor_scalar(first_rows[:, :], tile_no[:, 0:E], float(REGION), 0.0, ALU.mult, ALU.add
                                    ).then_inc(consts, 1)
            nc.gpsimd.tensor_scalar(rev[:, :], tile_no[:, 0:E], -1.0, float(E), ALU.mult, ALU.add).then_inc(consts, 1)
            nc.gpsimd.memset(tinfo[:, :, :], 0).then_inc(consts, 1)
            for g in range(NG):
                nc.gpsimd.memset(stq[g][:, :, :, :], 0.0).then_inc(consts, 1)
                nc.gpsimd.memset(stk[g][:, :, :], 0.0).then_inc(consts, 1)
                nc.gpsimd.memset(vaug[g][:, :, :, :], 0.0).then_inc(consts, 1)
            pool.wait_ge(consts, 15 + 3 * NG)
            for g in range(NG):
                nc.gpsimd.memset(vaug[g][:, :, :, DK:DK + 1], 1.0).then_inc(consts, 1)
            pool.wait_ge(consts, N_CONSTS)

            def split_step(bb, which, i):
                k = 5 * (2 * bb + which) + i
                if i:
                    pool.wait_ge(pool_chain, k)
                hi, mid, lo = (parts[:, which, n, :] for n in range(3))
                out_, a, c, op = ((rope[:, :], tcos[:, :], tsin[:, :], ALU.add), (hi, tcos[:, :], tsin[:, :], ALU.add),
                                  (rest[:, :], rope[:, :], hi, ALU.subtract), (mid, rope[:, :], hi, ALU.subtract),
                                  (lo, rest[:, :], mid, ALU.subtract))[i]
                nc.gpsimd.tensor_tensor(out_, a, c, op).then_inc(pool_chain, 1)
                if i == 4:
                    pool.wait_ge(pool_chain, k + 1)
                    pool.sem_inc(parts_done, 1)

            def settled():
                pool.sem_inc(pool_settled, 1)

            def lay_v(u, g):
                settled()
                nc.gpsimd.tensor_copy(vaug[g][:, :, :, 0:DK],
                                      vraw[:, :, G * DK * g:G * DK * (g + 1)].rearrange("p t (h c) -> p t h c", h=G)
                                      ).then_inc(vaug_done, 1)

            def split_max(b, steps, g, m):
                u = 0 if b is None else NG * b + g + 1
                taken(pool, b, steps, "MT", g, m)
                if b is not None:
                    pool.wait_ge(mrow_in[m], 48 * u)
                k = 3 * (2 * u + m)
                a, r, p = mrow[:, m, :], mrest[:, m, :], mparts[:, m]
                settled()
                nc.gpsimd.tensor_copy(p[:, 0, :], a).then_inc(max_chain, 1)
                pool.wait_ge(max_chain, k + 1)
                nc.gpsimd.tensor_tensor(r, a, p[:, 0, :], ALU.subtract).then_inc(max_chain, 1)
                nc.gpsimd.tensor_tensor(p[:, 1, :], a, p[:, 0, :], ALU.subtract).then_inc(max_chain, 1)
                pool.wait_ge(max_chain, k + 3)
                nc.gpsimd.tensor_tensor(p[:, 2, :], r, p[:, 1, :], ALU.subtract).then_inc(mparts_done, 1)

            for kind, g, m, n in before:
                if kind == "P" and m in (2, 4):
                    taken(pool, None, before, "P", 0, m)
                    for i in range(5):
                        split_step(0, m // 2 - 1, i)
                if kind == "P" and m == 5:
                    taken(pool, None, before, "P", 0, 5)
                    for g in range(NG):
                        lay_v(g, g)
                if kind == "MT":
                    split_max(None, before, -1, m)

            def batch(b, steps, last):
                for kind, g, m, n in steps:
                    if kind == "MT":
                        split_max(b, steps, g, m)
                    if kind == "E" and DIAGONAL[m]:
                        half, j, heads = E_ITEMS[m]
                        taken(pool, b, steps, "E", g, m)
                        w = width(half, j)
                        if len(heads) == G:
                            v = probs[m % RING][:, :, 0:2 * w].rearrange("p a (j q) -> p a j q", j=2)[:, :, :, 0:P]
                            pattern = [[0, 2], [0, 2], [1, P]]
                        else:
                            v = probs[m % RING][:, :, 0:P]
                            pattern = [[0, 2], [1, P]]
                        settled()
                        nc.gpsimd.affine_select(out=v, in_=v, compare_op=ALU.is_ge, fill=0.0, base=0,
                                                pattern=pattern, channel_multiplier=-1).then_inc(masked, 1)
                    if kind == "E" and not last and g in (1, 2) and 7 <= m < 12:
                        if m == 7:
                            taken(pool, b, steps, "P", g - 1, 2 * g) if g == 1 else taken(pool, b, steps, "P", 1, 4)
                            if g == 1:
                                pool.wait_ge(parts_out, 128 * (b + 1))
                        split_step(b + 1, g - 1, m - 7)
                    if kind == "L":
                        norm_squares(pool, b, res, sq)
                    if kind == "CT":
                        pool.wait_ge(rt_chain, RT * b + RT)
                        pool.wait_ge(x1_done, b + 1)
                        settled()
                        for t in range(NT):
                            for k in range(2):
                                nc.gpsimd.indirect_dma_start(
                                    x_rows, bass.IndirectOffsetOnAxis(ap=xr[:, k, t:t + 1], axis=0), x1[:, t, :], None
                                ).then_inc(scattered, 16)
                if not last:
                    taken(pool, b, steps, "P", 1, 5)
                    pool.wait_ge(pv_done, 1 + NPV * NG * (b + 1))
                    for g in range(NG):
                        lay_v(0, g)
                    pool.wait_ge(scattered, 16 * 2 * NT * (b + 1))
                    pool.sem_inc(x1_free, 1)

            every_batch(pool, batch)
        phase.close()
        attention.close()

        experts = ctx.enter_context(ExitStack())

        def sb(name, shape, dt=F32):
            return experts.enter_context(nc.sbuf_tensor(name, shape, dt))

        w2s = sb("w2s", [P, E, FC, D])
        LAG = 6
        xin = [sb(f"xin{i}", [P, D]) for i in range(3)]
        xinT = [sb(f"xinT{i}", [P, P]) for i in range(3)]
        hid = [sb(f"hid{i}", [P, F]) for i in range(3)]
        hidT = [sb(f"hidT{i}", [P, FC, P]) for i in range(3)]
        y = [sb(f"y{i}", [P, D]) for i in range(3)]
        yk = [sb(f"yk{i}", [P, 2, NT, D]) for i in range(2)]
        acc = [sb(f"acc{i}", [P, NT, D]) for i in range(2)]
        prod = sb("prod", [P, NT, D])
        sq = sb("sq2", [P, NT, D])
        x_ps, y_ps = opsum
        hid_ps = [slot[i][:, 0, :] for i in range(3)]
        hidT_ps = [slot[i][:, 1, :] for i in range(3)]

        tails_in = sem("tails_in")
        tile_in = [sem(f"tile_in{i}") for i in range(3)]
        x_turned = sem("x_turned")
        xT_out = sem("xT_out")
        hid_made = sem("hid_made")
        hid_out = sem("hid_out")
        hid_turned = sem("hid_turned")
        hidT_out = sem("hidT_out")
        y_made = sem("y_made")
        y_out = sem("y_out")
        y_stored = [sem(f"y_stored{i}") for i in range(3)]
        gathered = [sem(f"gathered{i}") for i in range(2)]
        mixed = sem("mixed")
        out_ready = sem("out_ready")
        out_stored = [sem(f"out_stored{i}") for i in range(2)]

        phase = ctx.enter_context(ExitStack())
        block = phase.enter_context(nc.Block())

        def tile_loop(eng, step, first, last):
            assert first % 3 == 0 and (NTILES - first) % 3 == 0
            for k in range(first):
                step(k, k % 3, k // 3)
            with eng.Fori(0, (NTILES - first) // 3) as i:
                for u in range(3):
                    step(3 * i + (first + u), u, i + first // 3)
            for k in range(NTILES, NTILES + last):
                step(k, k % 3, k // 3)

        def there(k):
            return not isinstance(k, int) or 0 <= k < NTILES

        @block.sync
        def _(sp):
            sp.dma_start(w2s[:, :, :, :], W2.rearrange("e (c p) h -> p e c h", p=P)).then_inc(we_in, 16)
            sp.wait_ge(scattered, 16 * 2 * T)
            for e in range(E):
                row = sp.value_load(tinfo[0:1, 2, e:e + 1], min_val=REGION * e, max_val=REGION * e + T * P)
                sp.dma_start(x_rows[bass.ds(row, P), :], zeros[:, :]).then_inc(tails_in, 16)
            sp.wait_ge(tails_in, 16 * E)
            sp.wait_ge(spare_in, 16 * (NTILES - 2 * T))

            def step(k, u, r):
                if there(k):
                    row = sp.value_load(tinfo[0:1, 1, bass.ds(k, 1)], min_val=0, max_val=(E + 1) * REGION - P)
                    if not (isinstance(k, int) and k < 3):
                        sp.wait_ge(x_turned, k - 2)
                    sp.dma_start(xin[u][:, :], x_rows[bass.ds(row, P), :]).then_inc(tile_in[u], 16)
                if there(k - LAG):
                    sp.wait_ge(y_out, k - LAG + 1)
                    sp.dma_start(y_rows[bass.ds((k - LAG) * P, P), :], y[u][:, :]).then_inc(y_stored[u], 16)

            tile_loop(sp, step, LAG, LAG)
            for b in range(B):
                sp.wait_ge(out_ready, b + 1)
                sp.dma_start(out[b].rearrange("(t p) d -> p t d", p=P), acc[b % 2][:, :, :]).then_inc(out_stored[b % 2], 16)
            for i in range(2):
                sp.wait_ge(out_stored[i], 16 * B // 2)

        @block.tensor
        def _(pe):
            pe.wait_ge(we_in, 32)

            def expert(k):
                return pe.value_load(tinfo[0:1, 0, bass.ds(k, 1)], min_val=0, max_val=E - 1)

            def second(k, u):
                e = expert(k)
                pe.wait_ge(hidT_out, k + 1)
                if not (isinstance(k, int) and k == 0):
                    pe.wait_ge(y_out, k)
                for c in range(FC):
                    mm = nc.tensor.matmul(y_ps[:, 0:D], hidT[u][:, c, :], w2s[:, bass.ds(e, 1), c, :],
                                          start=(c == 0), stop=(c == FC - 1))
                mm.then_inc(y_made, 1)

            def turn_hidden(k, u):
                pe.wait_ge(hid_out, k + 1)
                for c in range(FC):
                    mm = nc.tensor.transpose(hidT_ps[u][:, P * c:P * c + P], hid[u][:, P * c:P * c + P], ident[:, :])
                mm.then_inc(hid_turned, 1)

            def first(k, u):
                e = expert(k)
                pe.wait_ge(xT_out, k + 1)
                nc.tensor.matmul(hid_ps[u], xinT[u][:, :], w1s[:, bass.ds(e, 1), :], start=True, stop=True
                                 ).then_inc(hid_made, 1)

            def turn_x(k, u, r):
                pe.wait_ge(tile_in[u], 16 * (r + 1))
                if not (isinstance(k, int) and k == 0):
                    pe.wait_ge(xT_out, k)
                nc.tensor.transpose(x_ps[:, 0:P], xin[u][:, :], ident[:, :]).then_inc(x_turned, 1)

            def step(k, u, r):
                if there(k):
                    turn_x(k, u, r)
                if there(k - 1):
                    first(k - 1, (u - 1) % 3)
                if there(k - 2):
                    turn_hidden(k - 2, (u - 2) % 3)
                if there(k - 3):
                    second(k - 3, u)

            tile_loop(pe, step, 3, 3)

        @block.scalar
        def _(act):
            def step(k, u, r):
                if there(k):
                    act.wait_ge(x_turned, k + 1)
                    nc.scalar.activation(xinT[u][:, :], x_ps[:, 0:P], ACT.Copy).then_inc(xT_out, 1)
                if there(k - 1):
                    act.wait_ge(hid_made, k)
                    nc.scalar.activation(hid[(u - 1) % 3][:, :], hid_ps[(u - 1) % 3], ACT.Relu).then_inc(hid_out, 1)

            tile_loop(act, step, 3, 1)

        @block.vector
        def _(dve):
            def step(k, u, r):
                if there(k - 2):
                    dve.wait_ge(hid_turned, k - 1)
                    nc.vector.tensor_copy(hidT[(u - 2) % 3][:, :, :].rearrange("p c t -> p (c t)"),
                                          hidT_ps[(u - 2) % 3]).then_inc(hidT_out, 1)
                if there(k - 3):
                    dve.wait_ge(y_made, k - 2)
                    if not (isinstance(k, int) and k < LAG):
                        dve.wait_ge(y_stored[u], 16 * (r - 1))
                    nc.vector.tensor_copy(y[u][:, :], y_ps[:, 0:D]).then_inc(y_out, 1)

            tile_loop(dve, step, LAG, 3)

            v = nc.vector
            norm = layer_norm_on(dve, sq[:, :, :])
            for b in range(B):
                def link(i, ins):
                    ins.then_inc(mixed, 1)
                    dve.wait_ge(mixed, 4 * b + i)
                yy, total = yk[b % 2], acc[b % 2]
                dve.wait_ge(gathered[b % 2], 16 * 2 * NT * (b // 2 + 1))
                if b >= 2:
                    dve.wait_ge(out_stored[b % 2], 16 * (b // 2))
                link(1, v.tensor_tensor(prod[:, :, :], yy[:, 0], bc(gates[:, 0, tokens(b)]), ALU.mult))
                link(2, v.tensor_tensor(total[:, :, :], prod[:, :, :], xall[:, tokens(b), :], ALU.add))
                link(3, v.tensor_tensor(prod[:, :, :], yy[:, 1], bc(gates[:, 1, tokens(b)]), ALU.mult))
                link(4, v.tensor_tensor(total[:, :, :], total[:, :, :], prod[:, :, :], ALU.add))
                norm(B + b, total[:, :, :])
                v.tensor_tensor(total[:, :, :], total[:, :, :], bc(stat[:, 3, :]), ALU.mult).then_inc(out_ready, 1)

        @block.gpsimd
        def _(pool):
            for u in range(3):
                pool.wait_ge(y_stored[u], 16 * NTILES // 3)

            def gather(b):
                if b >= 2:
                    pool.wait_ge(mixed, 4 * (b - 1))
                for t in range(NT):
                    for k in range(2):
                        nc.gpsimd.indirect_dma_start(
                            yk[b % 2][:, k, t, :], None, y_rows,
                            bass.IndirectOffsetOnAxis(ap=y_row[:, k, NT * b + t:NT * b + t + 1], axis=0)
                        ).then_inc(gathered[b % 2], 16)

            gather(0)
            for b in range(B):
                if b + 1 < B:
                    gather(b + 1)
                norm_squares(pool, B + b, acc[b % 2][:, :, :], sq[:, :, :])

        phase.close()


def rope_tables(S):
    inv = (1.0 / 10000.0 ** (np.arange(0, DK, 2, dtype=np.float32) / np.float32(DK))).astype(np.float32)
    angles = np.outer(np.arange(S, dtype=np.float32), inv).astype(np.float32)
    lay = lambda t: np.ascontiguousarray(np.tile(np.repeat(t.astype(np.float32), 2, axis=-1).T, (H, 1)))
    return lay(np.cos(angles)), lay(np.sin(angles))


_INS = ["L0_attn_x", "L0_attn_Wq", "L0_attn_Wk", "L0_attn_Wv", "L0_attn_Wo", "L0_ffn_Wr", "L0_ffn_W1", "L0_ffn_W2"]


def kernel(**inputs):
    import concourse.bacc as bacc
    from concourse.bass_utils import run_bass_kernel_spmd as run

    nc = bacc.Bacc("TRN2", target_bir_lowering=False, num_devices=1)
    B, S, _ = inputs["L0_attn_x"].shape
    given = {n: np.ascontiguousarray(inputs[n]) for n in _INS}
    given["cos"], given["sin"] = rope_tables(S)
    arrays, args = {}, []
    for name, a in given.items():
        arrays[f"in_{name}_dram"] = a
        args.append(nc.dram_tensor(f"in_{name}_dram", a.shape, mybir.dt.from_np(a.dtype), kind="ExternalInput").ap())
    out = nc.dram_tensor("out_0_dram", (B, S, D), F32, kind="ExternalOutput").ap()
    build(nc, *args, out)
    r = run(nc, [arrays], core_ids=[0])
    return r.results[0]["out_0_dram"]
```

```python
from contextlib import ExitStack

import numpy as np

import concourse.bass as bass
from concourse import mybir

F32 = mybir.dt.float32
BF16 = mybir.dt.bfloat16
U32 = mybir.dt.uint32
ALU = mybir.AluOpType
ACT = mybir.ActivationFunctionType
AX = mybir.AxisListType

P = 128
D = 128
H = 16
DK = D // H
G = 4
NG = H // G
NEG = -3.0e38
EPS = 1e-5
SHIFT_AT = 96
SLOTS = 3
RING = 4


def score_items():
    out = []
    for half in range(2):
        for j in range(4 * half + 4):
            w = 512 - max(0, P * j - 512 * half)
            out += [(half, j, (0, 1, 2, 3))] if w <= 256 else [(half, j, (0, 1)), (half, j, (2, 3))]
    return out


def max_items():
    out = []
    for i in range(8):
        if i < 2:
            out.append((0, i, (0, 1, 2, 3)))
        elif i < 4:
            out += [(0, i, (0, 1)), (0, i, (2, 3))]
        else:
            out += [(1, i, (h,)) for h in range(G)]
    return out


E_ITEMS = score_items()
M_ITEMS = max_items()
NE, NM = len(E_ITEMS), len(M_ITEMS)
M_HALF = sum(1 for m in M_ITEMS if m[0] == 0)
E_HALF = sum(1 for e in E_ITEMS if e[0] == 0)
DIAGONAL = [j >= 4 * half for half, j, _ in E_ITEMS]
PV_GROUPS = sorted({(half, j) for half, j, _ in E_ITEMS})
PV_LAST = [max(n for n, e in enumerate(E_ITEMS) if e[:2] == g) for g in PV_GROUPS]
GROUP_OF = [PV_GROUPS.index(e[:2]) for e in E_ITEMS]
NPV = len(PV_GROUPS)


IN_SLOT = ("E", "M", "MT", "N", "P", "AT", "O", "XT", "LG", "CT", "D")
LN_STEPS, CHOICE_STEPS, RANK_STEPS = 6, 23, 16


def frame(db, g, maxima, extra, late=0):
    steps, m = [], 0
    for e in range(NE):
        if e < E_HALF + late:
            until = M_HALF * max(0, e + 1 - late) // E_HALF
        else:
            until = M_HALF + (NM - M_HALF) * (e + 1 - E_HALF - late) // (NE - E_HALF - late)
        while maxima and m < until:
            steps.append(("M", *maxima, m))
            m += 1
            if m in (M_HALF, NM):
                steps.append(("MT", *maxima, int(m == NM)))
        steps.append(("E", db, g, e))
        steps += extra.get(e, [])
    return steps


def output_steps(db, g, first):
    before = {} if first else {2: [("C", *unit_before(db, g), 1)], 4: [("N", *unit_before(db, g), 1)]}
    return {8: [("C", db, g, 0)], 10: [("N", db, g, 0)], **before}


def unit_before(db, g):
    return (db, g - 1) if g else (db - 1, NG - 1)


def merge(*plans):
    out = {}
    for plan in plans:
        for e, steps in plan.items():
            out[e] = out.get(e, []) + steps
    return out


def projection_plan():
    p = lambda *ms: [("P", 1, 0, m) for m in ms]
    split = lambda which, i: [("G", 1, which, i)]
    return {0: p(0), 1: p(1), 2: p(2), 4: split(0, 0), 5: p(3) + split(0, 1), 6: split(0, 2), 7: p(4) + split(0, 3),
            8: split(0, 4) + [("SQ", 1, 0, 0)], 9: split(1, 0), 10: split(1, 1), 11: split(1, 2) + p(5),
            12: split(1, 3), 13: split(1, 4) + [("SQ", 1, 0, 1), ("SK", 1, 0, 0)]}


def ending(db):
    one = lambda kind, m=0: (kind, db, 0, m)
    ln = [one("L", i) for i in range(LN_STEPS)]
    choice = [one("R", i) for i in range(CHOICE_STEPS)]
    rank = [one("K", i) for i in range(RANK_STEPS)]
    scatter = [one("S", t) for t in range(8)]
    frame0 = {5: [one("AT")], 7: [one("O")], 8: ln[0:3], 11: ln[3:5], 13: ln[5:6], 14: [one("XT")], 15: [one("LG")]}
    frame0 = merge(frame0, {16 + i: choice[4 * i:4 * i + 4] for i in range(4)})
    frame1 = {0: choice[16:20], 1: choice[20:23], 2: [one("CT")], 18: [one("F")]}
    frame1 = merge(frame1, {3 + i: rank[3 * i:3 * i + 3] for i in range(6)}, {9 + t: [scatter[t]] for t in range(8)})
    return frame0, frame1


def laid(*units):
    return [("V", 1, g, 0) for g in units]


def numbered(steps):
    out, n = [], 0
    steps = steps + [("D", 0, 0, i) for i in range(-sum(x[0] in IN_SLOT for x in steps) % SLOTS)]
    for step in steps:
        out.append((*step, n))
        n += step[0] in IN_SLOT
    return out, n


def units_2_3(last):
    if last:
        return frame(0, 2, (0, 3), output_steps(0, 2, False)) + frame(0, 3, None, output_steps(0, 3, False))
    return (frame(0, 2, (0, 3), merge(output_steps(0, 2, False), projection_plan()))
            + frame(0, 3, (1, 0), merge(output_steps(0, 3, False), {0: [("SK", 1, 1, 0)], 6: laid(0), 7: laid(1),
                                                                    8: laid(2), 10: [("SK", 1, 2, 0)]}), late=3))


def units_0_1(first):
    end0, end1 = ({}, {}) if first else ending(0)
    own = {} if first else {6: [("SK", 1, 3, 0)], 8: laid(3)}
    return (frame(1, 0, (1, 1), merge(output_steps(1, 0, first), end0, own))
            + frame(1, 1, (1, 2), merge(output_steps(1, 1, False), end1)))


def steps_before():
    steps = [("P", 1, 0, m) for m in range(3)] + [("G", 1, 0, i) for i in range(5)] + [("SQ", 1, 0, 0)]
    steps += [("P", 1, 0, 3), ("P", 1, 0, 4)] + [("G", 1, 1, i) for i in range(5)] + [("SQ", 1, 0, 1)]
    steps += [("SK", 1, g, 0) for g in range(NG)] + [("P", 1, 0, 5)] + laid(*range(NG))
    for m in range(NM):
        steps.append(("M", 1, 0, m))
        if m + 1 in (M_HALF, NM):
            steps.append(("MT", 1, 0, int(m + 1 == NM)))
    return numbered(steps + units_0_1(True))


def steps_of_batch(last):
    if not last:
        return numbered([("X", 1, 0, 0)] + units_2_3(False) + units_0_1(False))
    one = lambda kind, m=0: (kind, 0, 0, m)
    end = [("C", 0, NG - 1, 1), ("N", 0, NG - 1, 1), one("AT"), one("O")] + [one("L", i) for i in range(LN_STEPS)]
    end += [one("XT"), one("LG")] + [one("R", i) for i in range(CHOICE_STEPS)] + [one("CT")]
    end += [one("K", i) for i in range(RANK_STEPS)] + [one("S", t) for t in range(8)]
    return numbered(units_2_3(True) + end)


def build(nc, x, Wq, Wk, Wv, Wo, Wr, W1, W2, cos, sin, out):
    B, S, _ = x.shape
    E, _, F = W1.shape
    NT = S // P
    FC = F // P
    T = B * NT
    NTILES = 2 * T + E
    REGION = (T + 1) * P
    RT, RT_CNT = CHOICE_STEPS + RANK_STEPS, 17
    SCALE = float(DK) ** -0.5
    assert S == 1024 and D == P and F == 512 and E == 8

    before, n_before = steps_before()
    body, n_body = steps_of_batch(False)
    tail, _ = steps_of_batch(True)
    assert n_before % SLOTS == 0 and n_body % SLOTS == 0

    ctx = ExitStack()
    with ctx:
        def sb(name, shape, dt=F32):
            return ctx.enter_context(nc.sbuf_tensor(name, shape, dt))

        def sem(name):
            return ctx.enter_context(nc.semaphore(name))

        slot = [ctx.enter_context(nc.psum_tensor(f"slot{i}", [P, 2, 512], F32)) for i in range(SLOTS)]
        opsum = [ctx.enter_context(nc.psum_tensor(f"opsum{i}", [P, 512], F32)) for i in range(2)]

        ident = sb("ident", [P, P])
        identb = sb("identb", [P, P], BF16)
        maskb = sb("maskb", [P, P], BF16)
        before_b = sb("before_b", [P, P], BF16)
        onesb = sb("onesb", [P, P], BF16)
        neg_half = sb("neg_half", [P, NT])
        zeros = sb("zeros", [P, D])
        counts = sb("counts", [P, NTILES], mybir.dt.int32)
        first_rows = sb("first_rows", [P, E])
        rev = sb("rev", [P, E])
        tile_no = sb("tile_no", [P, NTILES])
        xall = sb("xall", [P, T, D])
        w1s = sb("w1s", [P, E, F])
        wr = sb("wr", [P, E])
        chosen = sb("chosen", [P, 2, T, E])
        gates = sb("gates", [P, 2, T])
        row_f = sb("row_f", [P, 2, T])
        y_row = sb("y_row", [P, 2, T], U32)
        run = sb("run", [P, NT + 1, E])
        stat = sb("stat", [P, 4, NT])
        tinfo = sb("tinfo", [P, 3, NTILES], mybir.dt.int32)
        x_rows = nc.dram_tensor("x_rows", ((E + 1) * REGION, D), F32).ap()
        y_rows = nc.dram_tensor("y_rows", (NTILES * P, D), F32).ap()

        attention = ctx.enter_context(ExitStack())

        def sb(name, shape, dt=F32):
            return attention.enter_context(nc.sbuf_tensor(name, shape, dt))

        wq, wk, wv, wo = (sb(n, [P, D]) for n in ("wq", "wk", "wv", "wo"))
        wqr, wkr = sb("wqr", [P, D]), sb("wkr", [P, D])
        cosT, sinT = sb("cosT", [P, S]), sb("sinT", [P, S])
        xT = sb("xT", [P, S])
        tcos, tsin = sb("tcos", [P, S]), sb("tsin", [P, S])
        rope = sb("rope", [P, S])
        rest = sb("rest", [P, S])
        parts = sb("parts", [P, 2, 3, S], BF16)
        vraw = sb("vraw", [P, NT, D])
        vaug = [sb(f"vaug{g}", [P, NT, G, 32]) for g in range(NG)]
        stq = [sb(f"stq{g}", [P, 2, G, 512], BF16) for g in range(NG)]
        stk = [sb(f"stk{g}", [P, G, S], BF16) for g in range(NG)]
        negm = sb("negm", [P, 2, 2, 16])
        mrow = sb("mrow", [16, 2, P])
        mrest = sb("mrest", [16, 2, P])
        mparts = sb("mparts", [16, 2, 3, P], BF16)
        probs = [sb(f"probs{i}", [P, 2, 512]) for i in range(RING)]
        osb = sb("osb", [P, 2, 512])
        rsum = sb("rsum", [P, 2, 4, G])
        attn = sb("attn", [P, NT, D])
        attnT = tcos
        res = rest[:, :].rearrange("p (t d) -> p t d", t=NT)
        sq = rope[:, :].rearrange("p (t d) -> p t d", t=NT)
        rt = [sb(f"rt{i}", [P, NT, E]) for i in range(5)]
        cntb = sb("cntb", [P, NT, E], BF16)
        before_it = sb("before_it", [P, 2, NT, E])
        rs = sb("rs", [P, 4, NT])
        tbl = sb("tbl", [P, 8, NTILES])
        x1 = sb("x1", [P, NT, D])
        xr = sb("xr", [P, 2, NT], U32)
        xnext = sb("xnext", [P, NT, D])

        q_dram = nc.dram_tensor("q_dram", (B, H, 3, DK, S), BF16).ap()
        k_dram = nc.dram_tensor("k_dram", (B, H, 5, DK, S), BF16).ap()

        x_in = sem("x_in")
        x_rest_in = sem("x_rest_in")
        ident_done = sem("ident_done")
        keys_zeroed = sem("keys_zeroed")
        zeroed = [sem(f"zeroed{g}") for g in range(NG)]
        w_in = sem("w_in")
        consts = sem("consts")
        wrot = sem("wrot")
        filled = [sem(f"filled{i}") for i in range(SLOTS)]
        left = [sem(f"left{i}") for i in range(SLOTS)]
        vaug_done = sem("vaug_done")
        split_chain = sem("split_chain")
        parts_out = sem("parts_out")
        stack_in = [sem(f"stack_in{g}") for g in range(NG)]
        mparts_done = sem("mparts_done")
        mrow_in = [sem(f"mrow_in{i}") for i in range(2)]
        masked = sem("masked")
        pv_done = sem("pv_done")
        osb_done = sem("osb_done")
        dve_chain = sem("dve_chain")
        dve_recip = sem("dve_recip")
        max_chain = sem("max_chain")
        pool_settled = sem("pool_settled")
        dve_settled = sem("dve_settled")
        xnow_done = sem("xnow_done")
        xnext_done = sem("xnext_done")
        ln_sq = sem("ln_sq")
        ln_var = sem("ln_var")
        ln_pow = sem("ln_pow")
        x1_kept = sem("x1_kept")
        x1_free = sem("x1_free")
        run_zero = sem("run_zero")
        x1_done = sem("x1_done")
        wr_in = sem("wr_in")
        we_in = sem("we_in")
        spare_in = sem("spare_in")
        rt_chain = sem("rt_chain")
        rt_exp = sem("rt_exp")
        rows_done = sem("rows_done")
        scattered = sem("scattered")
        table_done = sem("table_done")
        out_done = sem("out_done")
        N_CONSTS = 13 + 2 * NG

        phase = ctx.enter_context(ExitStack())
        block = phase.enter_context(nc.Block())

        def sections(eng, do):
            do(-1, before)
            with eng.Fori(0, B - 1) as b:
                do(b, body)
            do(B - 1, tail)

        def slot_of(b, n):
            if isinstance(b, int) and b < 0:
                return n % SLOTS, n // SLOTS
            return n % SLOTS, n_before // SLOTS + n // SLOTS + b * (n_body // SLOTS)

        def taken(eng, b, steps, kind, db, g, m):
            n = next(x[4] for x in steps if x[:4] == (kind, db, g, m))
            s, used = slot_of(b, n)
            eng.wait_ge(left[s], used + 1)

        def place(heads, h, w):
            return h % 2, (h // 2) * w if len(heads) == G else 0

        def width(half, j):
            return 512 - max(0, P * j - 512 * half)

        def tokens(b):
            return slice(NT * b, NT * b + NT) if isinstance(b, int) else bass.ds(b * NT, NT)

        def bc(s_):
            return s_.unsqueeze(2).to_broadcast([P, s_.shape[1], D])

        def norm_squares(pool, k, y, sq):
            pool.wait_ge(dve_chain, 4 * k + 3)
            nc.gpsimd.tensor_tensor(sq, y, y, ALU.mult).then_inc(ln_sq, 1)

        def norm_power(pool, k):
            pool.wait_ge(ln_var, k + 1)
            nc.gpsimd.tensor_tensor(stat[:, 3, :], stat[:, 0, :], neg_half[:, :], ALU.pow).then_inc(ln_pow, 1)

        def layer_norm(dve, k, y, sq, m):
            v = nc.vector
            if 1 <= m <= 2:
                dve.wait_ge(dve_chain, 4 * k + m)
            if m == 0:
                v.tensor_reduce(stat[:, 0, :], y, AX.X, ALU.add).then_inc(dve_chain, 1)
            elif m == 1:
                v.tensor_scalar(stat[:, 1, :], stat[:, 0, :], 1.0 / D, None, ALU.mult).then_inc(dve_chain, 1)
            elif m == 2:
                v.tensor_tensor(y, y, bc(stat[:, 1, :]), ALU.subtract).then_inc(dve_chain, 1)
            elif m == 3:
                dve.wait_ge(ln_sq, k + 1)
                v.tensor_reduce(stat[:, 2, :], sq, AX.X, ALU.add).then_inc(dve_chain, 1)
            elif m == 4:
                dve.wait_ge(dve_chain, 4 * k + 4)
                v.tensor_scalar(stat[:, 0, :], stat[:, 2, :], 1.0 / D, EPS, ALU.mult, ALU.add).then_inc(ln_var, 1)
            else:
                dve.wait_ge(ln_pow, k + 1)

        @block.sync
        def _(sp):
            xv = x.rearrange("b (t p) d -> p (b t) d", p=P)
            sp.dma_start(xall[:, 0:NT, :], xv[:, 0:NT, :]).then_inc(x_in, 16)
            for dst, src in ((wq, Wq), (wk, Wk), (wv, Wv), (wo, Wo), (cosT, cos), (sinT, sin)):
                sp.dma_start(dst[:, :], src).then_inc(w_in, 16)
            sp.dma_start(xall[:, NT:, :], xv[:, NT:, :]).then_inc(x_rest_in, 16)
            sp.dma_start(wr[:, :], Wr).then_inc(wr_in, 16)
            sp.dma_start(w1s[:, :, :], W1.rearrange("e h f -> h e f")).then_inc(we_in, 16)

            def store_parts(bb, which):
                sp.wait_ge(split_chain, 5 * (2 * bb + which + 1))
                dram = (q_dram, k_dram)[which]
                for at in range(dram.shape[2]):
                    sp.dma_start(dram[bb, :, at], parts[:, which, at % 3, :]).then_inc(parts_out, 16)

            def load_stack(bb, g):
                sp.wait_ge(parts_out, 128 * bb + 128)
                heads = slice(G * g, G * g + G)
                for r in range(3):
                    rows = slice(3 * DK * r, 3 * DK * (r + 1))
                    q_src = q_dram[bb, heads].rearrange("h n d s -> (n d) h s")
                    for half in range(2):
                        sp.dma_start(stq[g][rows, half, :, :],
                                     q_src[:, :, 512 * half:512 * half + 512]).then_inc(stack_in[g], 16)
                    sp.dma_start(stk[g][rows, :, :],
                                 k_dram[bb, heads, r:r + 3].rearrange("h n d s -> (n d) h s")).then_inc(stack_in[g], 16)

            def shift_rows(u, g, half):
                sp.wait_ge(mparts_done, 2 * u + half + 1)
                for part in range(3):
                    sp.dma_start(stq[g][SHIFT_AT + part:SHIFT_AT + part + 1, half, :, :],
                                 mparts[:, half, part, :]).then_inc(mrow_in[half], 16)

            for t in range(NTILES - 2 * T):
                if t == 0:
                    sp.wait_ge(consts, N_CONSTS)
                sp.dma_start(x_rows[E * REGION + P * t:E * REGION + P * (t + 1), :], zeros[:, :]).then_inc(spare_in, 16)

            def section(b, steps):
                for kind, db, g, m, n in steps:
                    if kind == "SQ":
                        store_parts(b + db, m)
                    if kind == "SK":
                        if steps is before:
                            sp.wait_ge(zeroed[g], 2)
                        else:
                            sp.wait_ge(pv_done, 1 + NPV * (NG * b + g + 1))
                        load_stack(b + db, g)
                    if kind == "MT":
                        shift_rows(NG * (b + db) + g, g, m)

            sections(sp, section)

        @block.tensor
        def _(pe):
            pe.sem_inc(pv_done, 1)
            pe.wait_ge(ident_done, 2)
            pe.wait_ge(x_in, 16)

            def pv_group(b, steps, db, g, n):
                half, j = PV_GROUPS[n]
                u = NG * (b + db) + g
                taken(pe, b, steps, "E", db, g, PV_LAST[n])
                if DIAGONAL[PV_LAST[n]]:
                    pe.wait_ge(masked, sum(DIAGONAL) * u + sum(DIAGONAL[:PV_LAST[n] + 1]))
                if j == 0:
                    if half == 0:
                        pe.wait_ge(vaug_done, u + 1)
                    pe.wait_ge(osb_done, 2 * u + 1 + half)
                w = width(half, j)
                for h in range(G):
                    k = next(k for k in range(NE) if GROUP_OF[k] == n and h in E_ITEMS[k][2])
                    bank, col = place(E_ITEMS[k][2], h, w)
                    mm = nc.tensor.matmul(opsum[half][32 * h:32 * h + 32, 512 - w:512], vaug[g][:, j, h, :],
                                          probs[k % RING][:, bank, col:col + w],
                                          start=(j == 0), stop=(j == 4 * half + 3), skip_group_check=True)
                mm.then_inc(pv_done, 1)

            def fill(b, steps, kind, db, g, m, n):
                s, used = slot_of(b, n)
                ps = slot[s]
                if not (steps is before and n < SLOTS):
                    pe.wait_ge(left[s], used)
                at = lambda t: ps[:, t // 4, P * (t % 4):P * (t % 4) + P]
                if kind == "P" and m == 0:
                    for t in range(NT):
                        src = xall[:, t, :] if steps is before else xnext[:, t, :]
                        if steps is not before and t == 0:
                            pe.wait_ge(xnext_done, b + 1)
                        mm = nc.tensor.transpose(at(t), src, ident[:, :])
                elif kind == "P":
                    if m == 1:
                        taken(pe, b, steps, "P", 1, 0, 0)
                        pe.wait_ge(w_in, 96)
                        pe.wait_ge(wrot, 4)
                    if m < 5:
                        w = (wq, wqr, wk, wkr)[m - 1]
                        for c in range(2):
                            mm = nc.tensor.matmul(ps[:, c, :], w[:, :], xT[:, 512 * c:512 * c + 512],
                                                  start=True, stop=True)
                    else:
                        for t in range(NT):
                            mm = nc.tensor.matmul(at(t), xT[:, P * t:P * t + P], wv[:, :], start=True, stop=True,
                                                  skip_group_check=True)
                elif kind == "M":
                    half, i, heads = M_ITEMS[m]
                    if m == 0:
                        pe.wait_ge(stack_in[g], 16 * 9 * (b + db + 1))
                        if steps is before and g == 0:
                            pe.wait_ge(consts, N_CONSTS)
                    keys = P * (i + 1)
                    for h in heads:
                        for c in range(0, keys, 512):
                            w = min(512, keys - c)
                            bank, col = (c // 512, 0) if len(heads) == 1 else place(heads, h, keys)
                            diag = c + w == keys
                            mm = nc.tensor.matmul(ps[:, bank, col:col + w], stq[g][0:SHIFT_AT, half, h, P * (i % 4):P * (i % 4) + P],
                                                  stk[g][0:SHIFT_AT, h, c:c + w], start=True, stop=not diag,
                                                  skip_group_check=True)
                            if diag:
                                mm = nc.tensor.matmul(ps[:, bank, col + w - P:col + w], identb[:, :], maskb[:, :],
                                                      start=False, stop=True, skip_group_check=True)
                elif kind == "MT":
                    taken(pe, b, steps, "M", db, g, NM - 1 if m else M_HALF - 1)
                    mm = nc.tensor.transpose(ps[0:16, 0, 0:P], negm[:, g % 2, m, :], ident[:, :])
                elif kind == "E":
                    half, j, heads = E_ITEMS[m]
                    if m in (0, E_HALF):
                        pe.wait_ge(mrow_in[half], 48 * (NG * (b + db) + g + 1))
                    w = width(half, j)
                    for h in heads:
                        bank, col = place(heads, h, w)
                        mm = nc.tensor.matmul(ps[:, bank, col:col + w], stk[g][:, h, P * j:P * j + P],
                                              stq[g][:, half, h, 512 - w:512],
                                              start=True, stop=True, skip_group_check=True)
                elif kind == "N":
                    pe.wait_ge(osb_done, 2 + 2 * (NG * (b + db) + g) + m + 1)
                    for t in range(4):
                        mm = nc.tensor.transpose(ps[:, 0, P * t:P * t + P], osb[:, m, P * t:P * t + P], ident[:, :])
                elif kind == "AT":
                    taken(pe, b, steps, "N", 0, NG - 1, 1)
                    for t in range(NT):
                        mm = nc.tensor.transpose(at(t), attn[:, t, :], ident[:, :])
                elif kind == "XT":
                    pe.wait_ge(x1_done, b + 1)
                    for t in range(NT):
                        mm = nc.tensor.transpose(at(t), x1[:, t, :], ident[:, :])
                elif kind == "LG":
                    taken(pe, b, steps, "XT", 0, 0, 0)
                    pe.wait_ge(wr_in, 16)
                    for t in range(NT):
                        mm = nc.tensor.matmul(ps[:, 0, E * t:E * t + E], attnT[:, P * t:P * t + P], wr[:, :],
                                              start=True, stop=True, skip_group_check=True)
                elif kind == "CT":
                    pe.wait_ge(rt_chain, RT * b + RT_CNT)
                    for c, w in enumerate((before_b, onesb)):
                        mm = nc.tensor.matmul(ps[:, 0, NT * E * c:NT * E * (c + 1)], w[:, :],
                                              cntb[:, :, :].rearrange("p t e -> p (t e)"), start=True, stop=True,
                                              skip_group_check=True)
                elif kind == "O":
                    taken(pe, b, steps, "AT", 0, 0, 0)
                    for t in range(NT):
                        mm = nc.tensor.matmul(at(t), attnT[:, P * t:P * t + P], wo[:, :], start=True, stop=True,
                                              skip_group_check=True)
                if kind == "D":
                    pe.sem_inc(filled[s], 1)
                else:
                    mm.then_inc(filled[s], 1)

            def section(b, steps):
                waiting = []
                for kind, db, g, m, n in steps:
                    if kind == "C":
                        while waiting and waiting[0] <= (db, g, NPV - 1 if m else 3):
                            pv_group(b, steps, *waiting.pop(0))
                    if kind not in IN_SLOT:
                        continue
                    fill(b, steps, kind, db, g, m, n)
                    if kind == "E":
                        now = NE * (NG * db + g) + m
                        while waiting and (NE * (NG * waiting[0][0] + waiting[0][1]) + PV_LAST[waiting[0][2]]
                                           <= now - 2):
                            pv_group(b, steps, *waiting.pop(0))
                        if m in PV_LAST:
                            waiting.append((db, g, PV_LAST.index(m)))
                for group in waiting:
                    pv_group(b, steps, *group)

            sections(pe, section)

        @block.scalar
        def _(act):
            act.sem_inc(osb_done, 2)

            def section(b, steps):
                for kind, db, g, m, n in steps:
                    s, used = slot_of(b, n)
                    flat = slot[s][:, :, :].rearrange("p a c -> p (a c)")
                    if kind == "P" and m == 0:
                        act.wait_ge(filled[s], used + 1)
                        nc.scalar.activation(xT[:, :], flat, ACT.Copy).then_inc(left[s], 1)
                    if kind == "P" and m == 5:
                        act.wait_ge(filled[s], used + 1)
                        if steps is not before:
                            act.wait_ge(vaug_done, NG * (b + 1))
                        nc.scalar.activation(vraw[:, :, :].rearrange("p a c -> p (a c)"), flat,
                                             ACT.Copy).then_inc(left[s], 1)
                    if kind == "E":
                        half, j, heads = E_ITEMS[m]
                        if not (steps is before and g == 0 and m < RING):
                            e = m - RING
                            act.wait_ge(pv_done, 2 + NPV * (NG * (b + db) + g + e // NE) + GROUP_OF[e % NE])
                        act.wait_ge(filled[s], used + 1)
                        wide = width(half, j) * len(heads) // 2
                        nc.scalar.activation(probs[m % RING][:, :, 0:wide], slot[s][:, :, 0:wide], ACT.Exp,
                                             scale=SCALE).then_inc(left[s], 1)
                    if kind == "C":
                        act.wait_ge(pv_done, 1 + NPV * (NG * (b + db) + g) + (NPV if m else 4))
                        nc.scalar.activation(osb[:, m, :], opsum[m][:, :], ACT.Copy).then_inc(osb_done, 1)
                    if kind == "G" and m in (1, 3):
                        act.wait_ge(split_chain, 5 * (2 * (b + db) + g) + m)
                        nc.scalar.activation(parts[:, g, m // 2, :], rope[:, :] if m == 1 else rest[:, :],
                                             ACT.Copy).then_inc(split_chain, 1)
                    if kind == "R" and m == 2:
                        act.wait_ge(rt_chain, RT * b + 2)
                        nc.scalar.activation(rt[1][:, :, :], rt[0][:, :, :], ACT.Exp).then_inc(rt_exp, 1)
                    if kind in ("AT", "XT"):
                        act.wait_ge(filled[s], used + 1)
                        nc.scalar.activation(attnT[:, :], flat, ACT.Copy).then_inc(left[s], 1)

            sections(act, section)

        @block.vector
        def _(dve):
            for g in range(NG):
                nc.vector.memset(stk[g][:, :, :].rearrange("p h k -> p (h k)").bitcast(F32), 0.0).then_inc(keys_zeroed, 1)
            dve.wait_ge(keys_zeroed, NG)
            for g in range(NG):
                nc.vector.memset(stk[g][SHIFT_AT:SHIFT_AT + 3, :, :], 1.0).then_inc(zeroed[g], 1)
            dve.wait_ge(w_in, 96)
            for w, r in ((wq, wqr), (wk, wkr)):
                pair = w[:, :].rearrange("p (c two) -> p c two", two=2)
                rot = r[:, :].rearrange("p (c two) -> p c two", two=2)
                nc.vector.tensor_scalar(rot[:, :, 0], pair[:, :, 1], -1.0, None, ALU.mult).then_inc(wrot, 1)
                nc.vector.tensor_copy(rot[:, :, 1], pair[:, :, 0]).then_inc(wrot, 1)

            def section(b, steps):
                for kind, db, g, m, n in steps:
                    s, used = slot_of(b, n)
                    ps = slot[s]
                    flat = ps[:, :, :].rearrange("p a c -> p (a c)")
                    if kind == "P" and 1 <= m < 5:
                        dve.wait_ge(filled[s], used + 1)
                        if m in (1, 3) and not (steps is before and m == 1):
                            which = (m - 3) // 2
                            dve.wait_ge(split_chain, 5 * (2 * (b + db) + which) + 1)
                        if m % 2:
                            nc.vector.tensor_tensor(tcos[:, :], flat, cosT[:, :], ALU.mult).then_inc(left[s], 1)
                        else:
                            nc.vector.tensor_tensor(tsin[:, :], flat, sinT[:, :], ALU.mult).then_inc(left[s], 1)
                    if kind == "M":
                        half, i, heads = M_ITEMS[m]
                        dve.wait_ge(filled[s], used + 1)
                        keys = P * (i + 1)
                        out_ = negm[:, g % 2, half, :].rearrange("p (j a q) -> p a j q", a=2, j=2)
                        q = i % 4
                        if len(heads) == G:
                            src = ps[:, :, 0:2 * keys].rearrange("p a (j k) -> p a j k", j=2)
                            dst = out_[:, :, :, q]
                        elif len(heads) == 2:
                            src = ps[:, :, 0:keys]
                            dst = out_[:, :, heads[0] // 2, q]
                        else:
                            src = flat[:, 0:keys]
                            dst = out_[:, heads[0] % 2, heads[0] // 2, q:q + 1]
                        nc.vector.tensor_reduce(dst, src, AX.X, ALU.max, negate=True).then_inc(left[s], 1)
                    if kind == "MT":
                        dve.wait_ge(filled[s], used + 1)
                        if not (steps is before and g == 0):
                            dve.wait_ge(mparts_done, 2 * (NG * (b + db) + g - 1) + m + 1)
                        nc.vector.tensor_copy(mrow[:, m, :], ps[0:16, 0, 0:P]).then_inc(left[s], 1)
                    if kind == "N":
                        u = NG * (b + db) + g
                        dve.wait_ge(filled[s], used + 1)
                        view = ps[:, 0, :].rearrange("p (t h c) -> p t h c", t=4, h=G)
                        nc.vector.reciprocal(rsum[:, m, :, :], view[:, :, :, DK]).then_inc(dve_recip, 1)
                        dve.wait_ge(dve_recip, 2 * u + m + 1)
                        nc.vector.tensor_tensor(
                            attn[:, 4 * m:4 * m + 4, G * DK * g:G * DK * (g + 1)].rearrange("p t (h c) -> p t h c", h=G),
                            view[:, :, :, 0:DK], rsum[:, m, :, :].unsqueeze(3).to_broadcast([P, 4, G, DK]),
                            ALU.mult).then_inc(left[s], 1)
                    if kind == "O":
                        dve.wait_ge(filled[s], used + 1)
                        nc.vector.tensor_tensor(res, ps[:, :, :].rearrange("p a (c d) -> p (a c) d", d=D),
                                                xall[:, tokens(b), :], ALU.add).then_inc(left[s], 1)
                    if kind == "L":
                        if m == 0:
                            taken(dve, b, steps, "O", 0, 0, 0)
                        layer_norm(dve, b, res, sq, m)
                        if m == LN_STEPS - 1:
                            dve.wait_ge(x1_free, b + 1)
                            nc.vector.tensor_tensor(x1[:, :, :], res, bc(stat[:, 3, :]), ALU.mult).then_inc(x1_done, 1)
                    if kind == "LG":
                        dve.wait_ge(filled[s], used + 1)
                        nc.vector.tensor_copy(rt[0][:, :, :].rearrange("p t e -> p (t e)"), ps[:, 0, 0:NT * E]
                                              ).then_inc(left[s], 1)
                    if kind == "R":
                        if m == 0:
                            taken(dve, b, steps, "LG", 0, 0, 0)
                        choose(b, m)
                        if m == 0:
                            dve.wait_ge(x1_done, b + 1)
                            settled()
                            nc.vector.tensor_copy(xall[:, tokens(b), :], x1[:, :, :]).then_inc(x1_kept, 1)
                    if kind == "CT":
                        dve.wait_ge(filled[s], used + 1)
                        nc.vector.tensor_copy(before_it[:, :, :, :].rearrange("p w t e -> p (w t e)"),
                                              ps[:, 0, 0:2 * NT * E]).then_inc(left[s], 1)
                    if kind == "K":
                        if m == 0:
                            taken(dve, b, steps, "CT", 0, 0, 0)
                        rank(b, m)
                    if kind == "X":
                        dve.wait_ge(x_rest_in, 16)
                        nc.vector.tensor_copy(xnext[:, :, :], xall[:, tokens(b + 1), :]).then_inc(xnext_done, 1)
                    if kind == "D":
                        dve.wait_ge(filled[s], used + 1)
                        dve.sem_inc(left[s], 1)

            def settled():
                dve.sem_inc(dve_settled, 1)

            def over_experts(s_):
                return s_.unsqueeze(2).to_broadcast([P, s_.shape[1], E])

            def over_tiles(s_):
                return s_.unsqueeze(1).to_broadcast([P, NT, E])

            def choose(b, m):
                v = nc.vector
                cut, ex, g, cand, tmp = (x[:, :, :] for x in rt)
                one, two = (chosen[:, k, tokens(b), :] for k in range(2))
                if m:
                    dve.wait_ge(rt_chain, RT * b + m)
                if m == 0:
                    ins = v.tensor_reduce(rs[:, 0, :], cut, AX.X, ALU.max)
                elif m == 1:
                    ins = v.tensor_tensor(cut, cut, over_experts(rs[:, 0, :]), ALU.subtract)
                elif m == 2:
                    dve.wait_ge(rt_exp, b + 1)
                    ins = v.tensor_reduce(rs[:, 1, :], ex, AX.X, ALU.add)
                elif m == 3:
                    ins = v.reciprocal(rs[:, 2, :], rs[:, 1, :])
                elif m == 4:
                    ins = v.tensor_tensor(g, ex, over_experts(rs[:, 2, :]), ALU.mult)
                elif m in (5, 11):
                    ins = v.tensor_reduce(rs[:, m // 11, :], g, AX.X, ALU.max)
                elif m in (6, 12):
                    ins = v.tensor_tensor(tmp, g, over_experts(rs[:, m // 12, :]), ALU.is_equal)
                elif m in (7, 13):
                    ins = v.tensor_tensor(cand, tmp, over_tiles(rev[:, :]), ALU.mult)
                elif m in (8, 14):
                    ins = v.tensor_reduce(rs[:, 3, :], cand, AX.X, ALU.max)
                elif m in (9, 15):
                    ins = v.tensor_tensor(cut if m == 9 else tmp, over_tiles(rev[:, :]), over_experts(rs[:, 3, :]),
                                          ALU.is_equal)
                elif m == 10:
                    ins = v.scalar_tensor_tensor(g, cut, -2.0, g, ALU.mult, ALU.add)
                elif m == 16:
                    ins = v.tensor_tensor(cntb[:, :, :], cut, tmp, ALU.add)
                elif m in (17, 18):
                    settled()
                    ins = v.tensor_copy(*((one, cut) if m == 17 else (two, tmp)))
                elif m == 19:
                    ins = v.tensor_tensor(rs[:, 2, :], rs[:, 0, :], rs[:, 1, :], ALU.add)
                elif m == 20:
                    ins = v.reciprocal(rs[:, 3, :], rs[:, 2, :])
                else:
                    ins = v.tensor_tensor(gates[:, m - 21, tokens(b)], rs[:, m - 21, :], rs[:, 3, :], ALU.mult)
                ins.then_inc(rt_chain, 1)

            def rank(b, m):
                v = nc.vector
                cut, ex, g, cand, tmp = (x[:, :, :] for x in rt)
                dve.wait_ge(rt_chain, RT * b + CHOICE_STEPS + m)
                if m < NT:
                    ins = v.tensor_tensor(run[:, m + 1, :], run[:, m, :], before_it[:, 1, m, :], ALU.add)
                elif m == 8:
                    ins = v.tensor_tensor(g, before_it[:, 0], run[:, 0:NT, :], ALU.add)
                elif m == 9:
                    ins = v.tensor_copy(run[:, 0, :], run[:, NT, :])
                elif m == 10:
                    ins = v.tensor_tensor(cand, g, over_tiles(first_rows[:, :]), ALU.add)
                elif m == 11:
                    ins = v.tensor_tensor(ex, cand, cut, ALU.mult)
                elif m == 12:
                    ins = v.tensor_tensor(g, cand, tmp, ALU.mult)
                elif m in (13, 14):
                    ins = v.tensor_reduce(row_f[:, m - 13, tokens(b)], ex if m == 13 else g, AX.X, ALU.add)
                else:
                    settled()
                    ins = v.tensor_copy(xr[:, :, :], row_f[:, :, tokens(b)])
                ins.then_inc(rt_chain, 1)

            def tables(dve):
                v = nc.vector
                done = [0]

                def step(ins):
                    done[0] += 1
                    ins.then_inc(table_done, 1)
                    dve.wait_ge(table_done, done[0])
                n_e = run[:, 0, :]
                share = tbl[:, 0, 0:E]
                n_tiles = tbl[:, 1, 0:E]
                end = tbl[:, 2, 0:E + 1]
                shift = tbl[:, 3, 0:E]
                is_over = tsin[:, 0:NTILES * E].rearrange("p (t e) -> p t e", e=E)
                over_tiles_of = sinT[:, 0:NTILES * E].rearrange("p (t e) -> p t e", e=E)
                begun = tsin[:, 0:E * T].rearrange("p (e t) -> p e t", e=E)
                mine = sinT[:, 0:T * E].rearrange("p (t e) -> p t e", e=E)
                wide = lambda s_, n: s_.unsqueeze(1).to_broadcast([P, n, s_.shape[1]])
                deep = lambda s_, n: s_.unsqueeze(2).to_broadcast([P, s_.shape[1], n])
                step(v.tensor_scalar(share, n_e, 1.0 / P, None, ALU.mult))
                step(v.tensor_tensor(begun, deep(share, T), wide(tile_no[:, 0:T], E), ALU.is_gt))
                step(v.tensor_reduce(n_tiles, begun, AX.X, ALU.add))
                step(v.memset(end[:, 0:1], 0.0))
                for e in range(E):
                    step(v.tensor_tensor(end[:, e + 1:e + 2], end[:, e:e + 1], n_tiles[:, e:e + 1], ALU.add))
                step(v.scalar_tensor_tensor(shift, end[:, 0:E], float(P), first_rows[:, :], ALU.mult, ALU.subtract))
                for k in range(2):
                    step(v.tensor_tensor(mine, chosen[:, k], wide(shift, T), ALU.mult))
                    step(v.tensor_reduce(tbl[:, 4, 0:T], mine, AX.X, ALU.add))
                    step(v.tensor_tensor(tbl[:, 5, 0:T], tbl[:, 4, 0:T], row_f[:, k, :], ALU.add))
                    step(v.tensor_copy(y_row[:, k, :], tbl[:, 5, 0:T]))
                step(v.tensor_tensor(is_over, deep(tile_no[:, :], E), wide(end[:, 1:E + 1], NTILES), ALU.is_ge))
                expert, tiles_over, row = (tbl[:, i, 0:NTILES] for i in (6, 7, 4))
                step(v.tensor_reduce(expert, is_over, AX.X, ALU.add))
                step(v.tensor_tensor(over_tiles_of, is_over, wide(n_tiles, NTILES), ALU.mult))
                step(v.tensor_reduce(tiles_over, over_tiles_of, AX.X, ALU.add))
                step(v.tensor_tensor(row, tile_no[:, :], tiles_over, ALU.subtract))
                step(v.tensor_scalar(tiles_over, expert, float(REGION), None, ALU.mult))
                step(v.scalar_tensor_tensor(row, row, float(P), tiles_over, ALU.mult, ALU.add))
                step(v.tensor_copy(tinfo[:, 1, :], row))
                step(v.tensor_scalar(expert, expert, float(E - 1), None, ALU.min))
                step(v.tensor_copy(tinfo[:, 0, :], expert))
                step(v.tensor_tensor(shift, first_rows[:, :], n_e, ALU.add))
                step(v.tensor_copy(tinfo[:, 2, 0:E], shift))

            nc.vector.memset(run[:, 0, :], 0.0).then_inc(run_zero, 1)
            dve.wait_ge(run_zero, 1)
            sections(dve, section)
            dve.wait_ge(rt_chain, RT * B)
            dve.wait_ge(x1_kept, B)
            tables(dve)

        @block.gpsimd
        def _(pool):
            pool.sem_inc(x1_free, 1)
            nc.gpsimd.memset(ident[:, :], 0.0).then_inc(ident_done, 1)
            pool.wait_ge(ident_done, 1)
            nc.gpsimd.affine_select(out=ident[:, :], in_=ident[:, :], compare_op=ALU.not_equal, fill=1.0, base=0,
                                    pattern=[[-1, P]], channel_multiplier=1).then_inc(ident_done, 1)
            for g in range(NG):
                nc.gpsimd.memset(stq[g][:, :, :, :].rearrange("p a h q -> p (a h q)").bitcast(F32), 0.0
                                 ).then_inc(zeroed[g], 1)

            def constants():
                nc.gpsimd.memset(maskb[:, :], 0.0).then_inc(consts, 1)
                pool.wait_ge(consts, 1)
                nc.gpsimd.affine_select(out=maskb[:, :], in_=maskb[:, :], compare_op=ALU.is_ge, fill=NEG, base=0,
                                        pattern=[[-1, P]], channel_multiplier=1).then_inc(consts, 1)
                pool.wait_ge(ident_done, 2)
                nc.gpsimd.tensor_copy(identb[:, :], ident[:, :]).then_inc(consts, 1)
                nc.gpsimd.memset(neg_half[:, :], -0.5).then_inc(consts, 1)
                nc.gpsimd.memset(zeros[:, :], 0.0).then_inc(consts, 1)
                nc.gpsimd.memset(onesb[:, :], 1.0).then_inc(consts, 1)
                nc.gpsimd.memset(before_b[:, :], 1.0).then_inc(consts, 1)
                nc.gpsimd.iota(counts[:, :], [[1, NTILES]], base=0, channel_multiplier=0).then_inc(consts, 1)
                pool.wait_ge(consts, 8)
                nc.gpsimd.affine_select(out=before_b[:, :], in_=before_b[:, :], compare_op=ALU.is_gt, fill=0.0, base=0,
                                        pattern=[[1, P]], channel_multiplier=-1).then_inc(consts, 1)
                nc.gpsimd.tensor_copy(tile_no[:, :], counts[:, :]).then_inc(consts, 1)
                pool.wait_ge(consts, 10)
                nc.gpsimd.tensor_scalar(first_rows[:, :], tile_no[:, 0:E], float(REGION), 0.0, ALU.mult, ALU.add
                                        ).then_inc(consts, 1)
                nc.gpsimd.tensor_scalar(rev[:, :], tile_no[:, 0:E], -1.0, float(E), ALU.mult, ALU.add
                                        ).then_inc(consts, 1)
                nc.gpsimd.memset(tinfo[:, :, :], 0).then_inc(consts, 1)
                for g in range(NG):
                    nc.gpsimd.memset(vaug[g][:, :, :, :], 0.0).then_inc(consts, 1)
                pool.wait_ge(consts, 13 + NG)
                for g in range(NG):
                    nc.gpsimd.memset(vaug[g][:, :, :, DK:DK + 1], 1.0).then_inc(consts, 1)
                pool.wait_ge(consts, N_CONSTS)

            def split_step(bb, which, m):
                if m:
                    pool.wait_ge(split_chain, 5 * (2 * bb + which) + m)
                if m == 0:
                    nc.gpsimd.tensor_tensor(rope[:, :], tcos[:, :], tsin[:, :], ALU.add).then_inc(split_chain, 1)
                elif m == 2:
                    nc.gpsimd.tensor_tensor(rest[:, :], rope[:, :], parts[:, which, 0, :], ALU.subtract
                                            ).then_inc(split_chain, 1)
                else:
                    nc.gpsimd.tensor_tensor(parts[:, which, 2, :], rest[:, :], parts[:, which, 1, :], ALU.subtract
                                            ).then_inc(split_chain, 1)

            def settled():
                pool.sem_inc(pool_settled, 1)

            def lay_v(g):
                settled()
                nc.gpsimd.tensor_copy(vaug[g][:, :, :, 0:DK],
                                      vraw[:, :, G * DK * g:G * DK * (g + 1)].rearrange("p t (h c) -> p t h c", h=G)
                                      ).then_inc(vaug_done, 1)

            def split_max(u, first, m):
                if not first:
                    pool.wait_ge(mrow_in[m], 48 * u)
                k = 3 * (2 * u + m)
                a, r, p = mrow[:, m, :], mrest[:, m, :], mparts[:, m]
                settled()
                nc.gpsimd.tensor_copy(p[:, 0, :], a).then_inc(max_chain, 1)
                pool.wait_ge(max_chain, k + 1)
                nc.gpsimd.tensor_tensor(r, a, p[:, 0, :], ALU.subtract).then_inc(max_chain, 1)
                nc.gpsimd.tensor_tensor(p[:, 1, :], a, p[:, 0, :], ALU.subtract).then_inc(max_chain, 1)
                pool.wait_ge(max_chain, k + 3)
                nc.gpsimd.tensor_tensor(p[:, 2, :], r, p[:, 1, :], ALU.subtract).then_inc(mparts_done, 1)

            def section(b, steps):
                for kind, db, g, m, n in steps:
                    if kind == "G" and m % 2 == 0:
                        if m == 0:
                            taken(pool, b, steps, "P", 1, 0, 2 * g + 2)
                            if steps is not before:
                                pool.wait_ge(parts_out, 128 * (b + db))
                        split_step(b + db, g, m)
                    if kind == "V":
                        if (steps is before or steps is body) and g == 0:
                            taken(pool, b, steps, "P", 1, 0, 5)
                            if steps is before:
                                constants()
                        if steps is not before:
                            pool.wait_ge(pv_done, 1 + NPV * (NG * b + g + 1))
                        lay_v(g)
                    if kind == "MT":
                        taken(pool, b, steps, "MT", db, g, m)
                        split_max(NG * (b + db) + g, steps is before and g == 0, m)
                    if kind == "E" and DIAGONAL[m]:
                        half, j, heads = E_ITEMS[m]
                        taken(pool, b, steps, "E", db, g, m)
                        w = width(half, j)
                        if len(heads) == G:
                            v = probs[m % RING][:, :, 0:2 * w].rearrange("p a (j q) -> p a j q", j=2)[:, :, :, 0:P]
                            pattern = [[0, 2], [0, 2], [1, P]]
                        else:
                            v = probs[m % RING][:, :, 0:P]
                            pattern = [[0, 2], [1, P]]
                        settled()
                        nc.gpsimd.affine_select(out=v, in_=v, compare_op=ALU.is_ge, fill=0.0, base=0,
                                                pattern=pattern, channel_multiplier=-1).then_inc(masked, 1)
                    if kind == "L" and m == 3:
                        norm_squares(pool, b, res, sq)
                    if kind == "L" and m == 5:
                        norm_power(pool, b)
                    if kind == "S":
                        if m == 0:
                            pool.wait_ge(rt_chain, RT * b + RT)
                            settled()
                        for k in range(2):
                            nc.gpsimd.indirect_dma_start(
                                x_rows, bass.IndirectOffsetOnAxis(ap=xr[:, k, m:m + 1], axis=0), x1[:, m, :], None
                            ).then_inc(scattered, 16)
                    if kind == "F":
                        pool.wait_ge(scattered, 16 * 2 * NT * (b + 1))
                        pool.sem_inc(x1_free, 1)

            sections(pool, section)
        phase.close()
        attention.close()

        experts = ctx.enter_context(ExitStack())

        def sb(name, shape, dt=F32):
            return experts.enter_context(nc.sbuf_tensor(name, shape, dt))

        w2s = sb("w2s", [P, E, FC, D])
        LAG = 6
        xin = [sb(f"xin{i}", [P, D]) for i in range(3)]
        xinT = [sb(f"xinT{i}", [P, P]) for i in range(3)]
        hid = [sb(f"hid{i}", [P, F]) for i in range(3)]
        hidT = [sb(f"hidT{i}", [P, FC, P]) for i in range(3)]
        y = [sb(f"y{i}", [P, D]) for i in range(3)]
        yk = [sb(f"yk{i}", [P, 2, NT, D]) for i in range(2)]
        acc = [sb(f"acc{i}", [P, NT, D]) for i in range(2)]
        prod = sb("prod", [P, NT, D])
        sq = sb("sq2", [P, NT, D])
        x_ps, y_ps = opsum
        hid_ps = [slot[i][:, 0, :] for i in range(3)]
        hidT_ps = [slot[i][:, 1, :] for i in range(3)]

        tails_in = sem("tails_in")
        tile_in = [sem(f"tile_in{i}") for i in range(3)]
        x_turned = sem("x_turned")
        xT_out = sem("xT_out")
        hid_made = sem("hid_made")
        hid_out = sem("hid_out")
        hid_turned = sem("hid_turned")
        hidT_out = sem("hidT_out")
        y_made = sem("y_made")
        y_out = sem("y_out")
        y_stored = [sem(f"y_stored{i}") for i in range(3)]
        gathered = [sem(f"gathered{i}") for i in range(2)]
        mixed = sem("mixed")
        out_ready = sem("out_ready")
        out_stored = [sem(f"out_stored{i}") for i in range(2)]

        phase = ctx.enter_context(ExitStack())
        block = phase.enter_context(nc.Block())

        def tile_loop(eng, step, first, last):
            assert first % 3 == 0 and (NTILES - first) % 3 == 0
            for k in range(first):
                step(k, k % 3, k // 3)
            with eng.Fori(0, (NTILES - first) // 3) as i:
                for u in range(3):
                    step(3 * i + (first + u), u, i + first // 3)
            for k in range(NTILES, NTILES + last):
                step(k, k % 3, k // 3)

        def there(k):
            return not isinstance(k, int) or 0 <= k < NTILES

        @block.sync
        def _(sp):
            sp.dma_start(w2s[:, :, :, :], W2.rearrange("e (c p) h -> p e c h", p=P)).then_inc(we_in, 16)
            sp.wait_ge(scattered, 16 * 2 * T)
            for e in range(E):
                row = sp.value_load(tinfo[0:1, 2, e:e + 1], min_val=REGION * e, max_val=REGION * e + T * P)
                sp.dma_start(x_rows[bass.ds(row, P), :], zeros[:, :]).then_inc(tails_in, 16)
            sp.wait_ge(tails_in, 16 * E)
            sp.wait_ge(spare_in, 16 * (NTILES - 2 * T))

            def step(k, u, r):
                if there(k):
                    row = sp.value_load(tinfo[0:1, 1, bass.ds(k, 1)], min_val=0, max_val=(E + 1) * REGION - P)
                    if not (isinstance(k, int) and k < 3):
                        sp.wait_ge(x_turned, k - 2)
                    sp.dma_start(xin[u][:, :], x_rows[bass.ds(row, P), :]).then_inc(tile_in[u], 16)
                if there(k - LAG):
                    sp.wait_ge(y_out, k - LAG + 1)
                    sp.dma_start(y_rows[bass.ds((k - LAG) * P, P), :], y[u][:, :]).then_inc(y_stored[u], 16)

            tile_loop(sp, step, LAG, LAG)
            for b in range(B):
                sp.wait_ge(out_ready, b + 1)
                sp.dma_start(out[b].rearrange("(t p) d -> p t d", p=P), acc[b % 2][:, :, :]).then_inc(out_stored[b % 2], 16)
            for i in range(2):
                sp.wait_ge(out_stored[i], 16 * B // 2)

        @block.tensor
        def _(pe):
            pe.wait_ge(we_in, 32)

            def expert(k):
                return pe.value_load(tinfo[0:1, 0, bass.ds(k, 1)], min_val=0, max_val=E - 1)

            def second(k, u):
                e = expert(k)
                pe.wait_ge(hidT_out, k + 1)
                if not (isinstance(k, int) and k == 0):
                    pe.wait_ge(y_out, k)
                for c in range(FC):
                    mm = nc.tensor.matmul(y_ps[:, 0:D], hidT[u][:, c, :], w2s[:, bass.ds(e, 1), c, :],
                                          start=(c == 0), stop=(c == FC - 1))
                mm.then_inc(y_made, 1)

            def turn_hidden(k, u):
                pe.wait_ge(hid_out, k + 1)
                for c in range(FC):
                    mm = nc.tensor.transpose(hidT_ps[u][:, P * c:P * c + P], hid[u][:, P * c:P * c + P], ident[:, :])
                mm.then_inc(hid_turned, 1)

            def first(k, u):
                e = expert(k)
                pe.wait_ge(xT_out, k + 1)
                nc.tensor.matmul(hid_ps[u], xinT[u][:, :], w1s[:, bass.ds(e, 1), :], start=True, stop=True
                                 ).then_inc(hid_made, 1)

            def turn_x(k, u, r):
                pe.wait_ge(tile_in[u], 16 * (r + 1))
                if not (isinstance(k, int) and k == 0):
                    pe.wait_ge(xT_out, k)
                nc.tensor.transpose(x_ps[:, 0:P], xin[u][:, :], ident[:, :]).then_inc(x_turned, 1)

            def step(k, u, r):
                if there(k):
                    turn_x(k, u, r)
                if there(k - 1):
                    first(k - 1, (u - 1) % 3)
                if there(k - 2):
                    turn_hidden(k - 2, (u - 2) % 3)
                if there(k - 3):
                    second(k - 3, u)

            tile_loop(pe, step, 3, 3)

        @block.scalar
        def _(act):
            def step(k, u, r):
                if there(k):
                    act.wait_ge(x_turned, k + 1)
                    nc.scalar.activation(xinT[u][:, :], x_ps[:, 0:P], ACT.Copy).then_inc(xT_out, 1)
                if there(k - 1):
                    act.wait_ge(hid_made, k)
                    nc.scalar.activation(hid[(u - 1) % 3][:, :], hid_ps[(u - 1) % 3], ACT.Relu).then_inc(hid_out, 1)

            tile_loop(act, step, 3, 1)

        @block.vector
        def _(dve):
            def step(k, u, r):
                if there(k - 2):
                    dve.wait_ge(hid_turned, k - 1)
                    nc.vector.tensor_copy(hidT[(u - 2) % 3][:, :, :].rearrange("p c t -> p (c t)"),
                                          hidT_ps[(u - 2) % 3]).then_inc(hidT_out, 1)
                if there(k - 3):
                    dve.wait_ge(y_made, k - 2)
                    if not (isinstance(k, int) and k < LAG):
                        dve.wait_ge(y_stored[u], 16 * (r - 1))
                    nc.vector.tensor_copy(y[u][:, :], y_ps[:, 0:D]).then_inc(y_out, 1)

            tile_loop(dve, step, LAG, 3)

            v = nc.vector
            for b in range(B):
                def link(i, ins):
                    ins.then_inc(mixed, 1)
                    dve.wait_ge(mixed, 4 * b + i)
                yy, total = yk[b % 2], acc[b % 2]
                dve.wait_ge(gathered[b % 2], 16 * 2 * NT * (b // 2 + 1))
                if b >= 2:
                    dve.wait_ge(out_stored[b % 2], 16 * (b // 2))
                link(1, v.tensor_tensor(prod[:, :, :], yy[:, 0], bc(gates[:, 0, tokens(b)]), ALU.mult))
                link(2, v.tensor_tensor(total[:, :, :], prod[:, :, :], xall[:, tokens(b), :], ALU.add))
                link(3, v.tensor_tensor(prod[:, :, :], yy[:, 1], bc(gates[:, 1, tokens(b)]), ALU.mult))
                link(4, v.tensor_tensor(total[:, :, :], total[:, :, :], prod[:, :, :], ALU.add))
                for m in range(LN_STEPS):
                    layer_norm(dve, B + b, total[:, :, :], sq[:, :, :], m)
                v.tensor_tensor(total[:, :, :], total[:, :, :], bc(stat[:, 3, :]), ALU.mult).then_inc(out_ready, 1)

        @block.gpsimd
        def _(pool):
            for u in range(3):
                pool.wait_ge(y_stored[u], 16 * NTILES // 3)

            def gather(b):
                if b >= 2:
                    pool.wait_ge(mixed, 4 * (b - 1))
                for t in range(NT):
                    for k in range(2):
                        nc.gpsimd.indirect_dma_start(
                            yk[b % 2][:, k, t, :], None, y_rows,
                            bass.IndirectOffsetOnAxis(ap=y_row[:, k, NT * b + t:NT * b + t + 1], axis=0)
                        ).then_inc(gathered[b % 2], 16)

            gather(0)
            for b in range(B):
                if b + 1 < B:
                    gather(b + 1)
                norm_squares(pool, B + b, acc[b % 2][:, :, :], sq[:, :, :])
                norm_power(pool, B + b)

        phase.close()


def rope_tables(S):
    inv = (1.0 / 10000.0 ** (np.arange(0, DK, 2, dtype=np.float32) / np.float32(DK))).astype(np.float32)
    angles = np.outer(np.arange(S, dtype=np.float32), inv).astype(np.float32)
    lay = lambda t: np.ascontiguousarray(np.tile(np.repeat(t.astype(np.float32), 2, axis=-1).T, (H, 1)))
    return lay(np.cos(angles)), lay(np.sin(angles))


_INS = ["L0_attn_x", "L0_attn_Wq", "L0_attn_Wk", "L0_attn_Wv", "L0_attn_Wo", "L0_ffn_Wr", "L0_ffn_W1", "L0_ffn_W2"]


def kernel(**inputs):
    import concourse.bacc as bacc
    from concourse.bass_utils import run_bass_kernel_spmd as run

    nc = bacc.Bacc("TRN2", target_bir_lowering=False, num_devices=1)
    B, S, _ = inputs["L0_attn_x"].shape
    given = {n: np.ascontiguousarray(inputs[n]) for n in _INS}
    given["cos"], given["sin"] = rope_tables(S)
    arrays, args = {}, []
    for name, a in given.items():
        arrays[f"in_{name}_dram"] = a
        args.append(nc.dram_tensor(f"in_{name}_dram", a.shape, mybir.dt.from_np(a.dtype), kind="ExternalInput").ap())
    out = nc.dram_tensor("out_0_dram", (B, S, D), F32, kind="ExternalOutput").ap()
    build(nc, *args, out)
    r = run(nc, [arrays], core_ids=[0])
    return r.results[0]["out_0_dram"]
```

```python
from contextlib import ExitStack

import numpy as np

import concourse.bass as bass
from concourse import mybir

F32 = mybir.dt.float32
BF16 = mybir.dt.bfloat16
U32 = mybir.dt.uint32
ALU = mybir.AluOpType
ACT = mybir.ActivationFunctionType
AX = mybir.AxisListType

P = 128
D = 128
H = 16
DK = D // H
G = 4
NG = H // G
NEG = -3.0e38
EPS = 1e-5
SHIFT_AT = 96
SLOTS = 3
RING = 4


def score_items():
    out = []
    for half in range(2):
        for j in range(4 * half + 4):
            w = 512 - max(0, P * j - 512 * half)
            out += [(half, j, (0, 1, 2, 3))] if w <= 256 else [(half, j, (0, 1)), (half, j, (2, 3))]
    return out


def max_items():
    out = []
    for i in range(8):
        if i < 2:
            out.append((0, i, (0, 1, 2, 3)))
        elif i < 4:
            out += [(0, i, (0, 1)), (0, i, (2, 3))]
        else:
            out += [(1, i, (h,)) for h in range(G)]
    return out


E_ITEMS = score_items()
M_ITEMS = max_items()
NE, NM = len(E_ITEMS), len(M_ITEMS)
M_HALF = sum(1 for m in M_ITEMS if m[0] == 0)
E_HALF = sum(1 for e in E_ITEMS if e[0] == 0)
DIAGONAL = [j >= 4 * half for half, j, _ in E_ITEMS]
PV_GROUPS = sorted({(half, j) for half, j, _ in E_ITEMS})
PV_LAST = [max(n for n, e in enumerate(E_ITEMS) if e[:2] == g) for g in PV_GROUPS]
GROUP_OF = [PV_GROUPS.index(e[:2]) for e in E_ITEMS]
PV_PARTS = [1 if j == 0 else GROUP_OF.count(n) for n, (_, j) in enumerate(PV_GROUPS)]
NPV = len(PV_GROUPS)


IN_SLOT = ("E", "M", "MT", "N", "P", "AT", "O", "XT", "LG", "CT", "D")
LEAD = 7
M_FIXED = 220
LN_STEPS, CHOICE_STEPS, RANK_STEPS = 6, 24, 16


def maxima_of(db, g):
    items = [("M", db, g, m) for m in range(NM)]
    return items[:M_HALF + 2] + [("MT", db, g, 0)] + items[M_HALF + 2:]


def frame(db, g, maxima, extra, start=0, stop=NE, late=0):
    e_work = [0 if e < start + late else (512 - max(0, P * j - 512 * half)) * len(heads)
              for e, (half, j, heads) in enumerate(E_ITEMS[:stop])]
    m_work = [P * (M_ITEMS[m][1] + 1) * len(M_ITEMS[m][2]) + M_FIXED if kind == "M" else M_FIXED
              for kind, _, _, m in maxima]
    steps, n = [], 0
    for e in range(start, stop):
        share = sum(e_work[start:e + 1]) / sum(e_work[start:])
        while n < len(maxima) and sum(m_work[:n + 1]) <= share * sum(m_work) + 1:
            steps.append(maxima[n])
            n += 1
        steps.append(("E", db, g, e))
        steps += extra.get(e, [])
    return steps


def output_steps(db, g, first):
    before = {} if first else {2: [("C", *unit_before(db, g), 1)], 4: [("N", *unit_before(db, g), 1)]}
    if (db, g) == (1, 1):
        before[NE - 1] = [("MT", 1, 2, 1)]
    if not first and (db, g) != (0, 2):
        before[1] = [("MT", db, g, 1)]
    return {8: [("C", db, g, 0)], 10: [("N", db, g, 0)], **before}


def unit_before(db, g):
    return (db, g - 1) if g else (db - 1, NG - 1)


def merge(*plans):
    out = {}
    for plan in plans:
        for e, steps in plan.items():
            out[e] = out.get(e, []) + steps
    return out


def projection_plan():
    p = lambda *ms: [("P", 1, 0, m) for m in ms]
    split = lambda which, i: [("G", 1, which, i)]
    return {0: p(0), 1: p(1), 2: p(2), 4: split(0, 0), 5: p(3) + split(0, 1), 6: split(0, 2), 7: p(4) + split(0, 3),
            8: split(0, 4) + [("SQ", 1, 0, 0)], 9: split(1, 0), 10: split(1, 1), 11: split(1, 2) + p(5),
            12: split(1, 3), 13: split(1, 4) + [("SQ", 1, 0, 1), ("SK", 1, 0, 0)]}


def ending(db):
    one = lambda kind, m=0: (kind, db, 0, m)
    ln = [one("L", i) for i in range(LN_STEPS)]
    choice = [one("R", i) for i in range(CHOICE_STEPS)]
    rank = [one("K", i) for i in range(RANK_STEPS)]
    scatter = [one("S", t) for t in range(16)]
    frame0 = {5: [one("AT")], 7: [one("O")], 8: ln[0:3], 11: ln[3:5], 13: ln[5:6], 15: [one("XT")], 16: [one("LG")],
              17: choice[0:6], 18: choice[6:12], 19: choice[12:18]}
    frame1 = merge({0: choice[18:24], 2: [one("CT")], NE - 1: [one("F")]},
                   {3 + i: rank[4 * i:4 * i + 4] for i in range(4)},
                   {6 + i: scatter[2 * i:2 * i + 2] for i in range(4)}, {10 + i: [scatter[8 + i]] for i in range(8)})
    return frame0, frame1


def laid(*units):
    return [("V", 1, g, 0) for g in units]


def numbered(steps):
    out, n = [], 0
    steps = steps + [("D", 0, 0, i) for i in range(-sum(x[0] in IN_SLOT for x in steps) % SLOTS)]
    for step in steps:
        out.append((*step, n))
        n += step[0] in IN_SLOT
    return out, n


def units_2_3(last):
    if last:
        weights = {5: [("W2", 0, 0, 0)]}
        return frame(0, 2, maxima_of(0, 3), merge(output_steps(0, 2, False), weights)) + frame(0, 3, [], output_steps(0, 3, False))
    return (frame(0, 2, maxima_of(0, 3), merge(output_steps(0, 2, False), projection_plan()))
            + frame(0, 3, maxima_of(1, 0), merge(output_steps(0, 3, False), {
                0: [("SK", 1, 1, 0)], 6: laid(0), 7: laid(1), 8: laid(2), 10: [("SK", 1, 2, 0)]}), late=4))


def units_0_1():
    end0, end1 = ending(0)
    own = {6: [("SK", 1, 3, 0)], 8: laid(3)}
    return (frame(1, 0, maxima_of(1, 1), merge(output_steps(1, 0, False), end0, own))
            + frame(1, 1, maxima_of(1, 2), merge(output_steps(1, 1, False), end1)))


def steps_before():
    steps = [("P", 1, 0, m) for m in range(3)] + [("G", 1, 0, i) for i in range(5)] + [("SQ", 1, 0, 0)]
    steps += [("P", 1, 0, 3), ("P", 1, 0, 4)] + [("G", 1, 1, i) for i in range(5)] + [("SQ", 1, 0, 1)]
    steps += [("SK", 1, g, 0) for g in range(NG)] + [("P", 1, 0, 5)] + laid(*range(NG))
    first, second = maxima_of(1, 0), maxima_of(1, 1)
    extra = output_steps(1, 0, True)
    steps += first[:M_HALF + LEAD]
    steps += frame(1, 0, first[M_HALF + LEAD:], extra, stop=E_HALF)
    steps += second[:3] + [("MT", 1, 0, 1)] + second[3:LEAD]
    steps += frame(1, 0, second[LEAD:], extra, start=E_HALF)
    steps += frame(1, 1, maxima_of(1, 2), output_steps(1, 1, False))
    return numbered(steps)


def steps_of_batch(last):
    if not last:
        return numbered([("X", 1, 0, 0)] + units_2_3(False) + units_0_1())
    one = lambda kind, m=0: (kind, 0, 0, m)
    end = [("C", 0, NG - 1, 1), ("N", 0, NG - 1, 1), one("AT"), one("O")] + [one("L", i) for i in range(LN_STEPS)]
    end += [one("XT"), one("LG")] + [one("R", i) for i in range(CHOICE_STEPS)] + [one("CT")]
    end += [one("K", i) for i in range(RANK_STEPS)] + [one("S", t) for t in range(16)]
    return numbered(units_2_3(True) + end)


def build(nc, x, Wq, Wk, Wv, Wo, Wr, W1, W2, cos, sin, out):
    B, S, _ = x.shape
    E, _, F = W1.shape
    NT = S // P
    FC = F // P
    T = B * NT
    NTILES = 2 * T + E
    REGION = (T + 1) * P
    RT, RT_CNT = CHOICE_STEPS + RANK_STEPS, 17
    DW = D + 2
    SCALE = float(DK) ** -0.5
    assert S == 1024 and D == P and F == 512 and E == 8

    before, n_before = steps_before()
    body, n_body = steps_of_batch(False)
    tail, _ = steps_of_batch(True)
    assert n_before % SLOTS == 0 and n_body % SLOTS == 0

    ctx = ExitStack()
    with ctx:
        def sb(name, shape, dt=F32):
            return ctx.enter_context(nc.sbuf_tensor(name, shape, dt))

        def sem(name):
            return ctx.enter_context(nc.semaphore(name))

        slot = [ctx.enter_context(nc.psum_tensor(f"slot{i}", [P, 2, 512], F32)) for i in range(SLOTS)]
        opsum = [ctx.enter_context(nc.psum_tensor(f"opsum{i}", [P, 512], F32)) for i in range(2)]

        ident = sb("ident", [P, P])
        identb = sb("identb", [P, P], BF16)
        maskb = sb("maskb", [P, P], BF16)
        before_b = sb("before_b", [P, P], BF16)
        onesb = sb("onesb", [P, P], BF16)
        neg_half = sb("neg_half", [P, NT])
        blank = sb("blank", [P, NTILES - 2 * T + E, DW])
        counts = sb("counts", [P, NTILES], mybir.dt.int32)
        first_rows = sb("first_rows", [P, E])
        rev = sb("rev", [P, E])
        y_row = sb("y_row", [P, 2, NT], mybir.dt.int32)
        tile_no = sb("tile_no", [P, NTILES])
        xall = sb("xall", [P, T, D])
        w1s = sb("w1s", [P, E, F])
        wr = sb("wr", [P, E])
        run = sb("run", [P, NT + 1, E])
        stat = sb("stat", [P, 4, NT])
        tinfo = sb("tinfo", [P, 3, NTILES], mybir.dt.int32)
        x_rows = nc.dram_tensor("x_rows", ((E + 1) * REGION, DW), F32).ap()
        y_rows = nc.dram_tensor("y_rows", ((NTILES + E) * P, D), F32).ap()

        w2s = sb("w2s", [P, E, FC, D])

        attention = ctx.enter_context(ExitStack())

        def sb(name, shape, dt=F32):
            return attention.enter_context(nc.sbuf_tensor(name, shape, dt))

        wq, wk, wv, wo = (sb(n, [P, D]) for n in ("wq", "wk", "wv", "wo"))
        wqr, wkr = sb("wqr", [P, D]), sb("wkr", [P, D])
        cosT, sinT = sb("cosT", [P, S]), sb("sinT", [P, S])
        xT = sb("xT", [P, S])
        tcos, tsin = sb("tcos", [P, S]), sb("tsin", [P, S])
        wide_rope = sb("wide_rope", [P, NT * DW])
        rope = wide_rope[:, 0:S]
        rest = sb("rest", [P, S])
        parts = sb("parts", [P, 2, 3, S], BF16)
        vraw = sb("vraw", [P, NT, D])
        xnext = vraw
        vaug = [sb(f"vaug{g}", [P, NT, G, 32]) for g in range(NG)]
        stq = [sb(f"stq{g}", [P, 2, G, 512], BF16) for g in range(NG)]
        early = w2s[:, :, :, :].rearrange("p e c d -> p (e c d)").bitcast(BF16)
        stk = [early[:, G * S * g:G * S * (g + 1)].rearrange("p (h k) -> p h k", h=G) for g in range(2)]
        stk += [sb(f"stk{g}", [P, G, S], BF16)[:, :, :] for g in range(2, NG)]
        negm = sb("negm", [P, 2, 2, 16])
        mrow = sb("mrow", [16, 2, P])
        mrest = sb("mrest", [16, 2, P])
        mparts = sb("mparts", [16, 2, 3, P], BF16)
        probs = [sb(f"probs{i}", [P, 2, 512]) for i in range(RING)]
        osb = sb("osb", [P, 2, 512])
        rsum = sb("rsum", [P, 2, 4, G])
        attn = sb("attn", [P, NT, D])
        attnT = tcos
        res = rest[:, :].rearrange("p (t d) -> p t d", t=NT)
        sq = rope.rearrange("p (t d) -> p t d", t=NT)
        rt = [sb(f"rt{i}", [P, NT, E]) for i in range(5)]
        cntb = sb("cntb", [P, NT, E], BF16)
        before_it = sb("before_it", [P, 2, NT, E])
        rs = sb("rs", [P, 4, NT])
        row_f = sb("row_f", [P, 2, NT])
        tbl = sb("tbl", [P, 8, NTILES])
        x1 = (sb("x1", [P, NT, DW]), wide_rope[:, :].rearrange("p (t d) -> p t d", t=NT))
        y_of = sb("y_of", [P, 2, NT])
        xr = sb("xr", [P, 2, NT], U32)

        q_dram = nc.dram_tensor("q_dram", (B, H, 3, DK, S), BF16).ap()
        k_dram = nc.dram_tensor("k_dram", (B, H, 5, DK, S), BF16).ap()

        x_in = sem("x_in")
        x_rest_in = sem("x_rest_in")
        ident_done = sem("ident_done")
        keys_zeroed = sem("keys_zeroed")
        zeroed = [sem(f"zeroed{g}") for g in range(NG)]
        w_in = sem("w_in")
        consts = sem("consts")
        wrot = sem("wrot")
        filled = [sem(f"filled{i}") for i in range(SLOTS)]
        left = [sem(f"left{i}") for i in range(SLOTS)]
        vaug_done = sem("vaug_done")
        split_chain = sem("split_chain")
        parts_out = sem("parts_out")
        stack_in = [sem(f"stack_in{g}") for g in range(NG)]
        mparts_done = sem("mparts_done")
        mrow_in = [sem(f"mrow_in{i}") for i in range(2)]
        masked = sem("masked")
        pv_done = sem("pv_done")
        osb_done = sem("osb_done")
        dve_chain = sem("dve_chain")
        dve_recip = sem("dve_recip")
        max_chain = sem("max_chain")
        pool_settled = sem("pool_settled")
        dve_settled = sem("dve_settled")
        act_settled = sem("act_settled")
        xnext_done = sem("xnext_done")
        ln_sq = sem("ln_sq")
        ln_var = sem("ln_var")
        ln_pow = sem("ln_pow")
        x1_twin = sem("x1_twin")
        x1_kept = sem("x1_kept")
        x1_free = sem("x1_free")
        run_zero = sem("run_zero")
        x1_done = sem("x1_done")
        wr_in = sem("wr_in")
        we_in = sem("we_in")
        spare_in = sem("spare_in")
        rt_chain = sem("rt_chain")
        rt_exp = sem("rt_exp")
        scattered = sem("scattered")
        table_done = sem("table_done")
        tails_in = sem("tails_in")
        w2_in = sem("w2_in")
        N_TABLE = 17 + E
        N_CONSTS = 16 + 2 * NG

        phase = ctx.enter_context(ExitStack())
        block = phase.enter_context(nc.Block())

        def sections(eng, do):
            do(-1, before)
            with eng.Fori(0, B - 1) as b:
                do(b, body)
            do(B - 1, tail)

        def slot_of(b, n):
            if isinstance(b, int) and b < 0:
                return n % SLOTS, n // SLOTS
            return n % SLOTS, n_before // SLOTS + n // SLOTS + b * (n_body // SLOTS)

        def taken(eng, b, steps, kind, db, g, m):
            n = next(x[4] for x in steps if x[:4] == (kind, db, g, m))
            s, used = slot_of(b, n)
            eng.wait_ge(left[s], used + 1)

        def place(heads, h, w):
            return h % 2, (h // 2) * w if len(heads) == G else 0

        def width(half, j):
            return 512 - max(0, P * j - 512 * half)

        def tokens(b):
            return slice(NT * b, NT * b + NT) if isinstance(b, int) else bass.ds(b * NT, NT)

        def bc(s_):
            return s_.unsqueeze(2).to_broadcast([P, s_.shape[1], D])

        def norm_squares(pool, k, y, sq):
            pool.wait_ge(dve_chain, 4 * k + 3)
            nc.gpsimd.tensor_tensor(sq, y, y, ALU.mult).then_inc(ln_sq, 1)

        def norm_power(pool, k):
            pool.wait_ge(ln_var, k + 1)
            nc.gpsimd.tensor_tensor(stat[:, 3, :], stat[:, 0, :], neg_half[:, :], ALU.pow).then_inc(ln_pow, 1)

        def layer_norm(dve, k, y, sq, m):
            v = nc.vector
            if 1 <= m <= 2:
                dve.wait_ge(dve_chain, 4 * k + m)
            if m == 0:
                v.tensor_reduce(stat[:, 0, :], y, AX.X, ALU.add).then_inc(dve_chain, 1)
            elif m == 1:
                v.tensor_scalar(stat[:, 1, :], stat[:, 0, :], 1.0 / D, None, ALU.mult).then_inc(dve_chain, 1)
            elif m == 2:
                v.tensor_tensor(y, y, bc(stat[:, 1, :]), ALU.subtract).then_inc(dve_chain, 1)
            elif m == 3:
                dve.wait_ge(ln_sq, k + 1)
                v.tensor_reduce(stat[:, 2, :], sq, AX.X, ALU.add).then_inc(dve_chain, 1)
            elif m == 4:
                dve.wait_ge(dve_chain, 4 * k + 4)
                v.tensor_scalar(stat[:, 0, :], stat[:, 2, :], 1.0 / D, EPS, ALU.mult, ALU.add).then_inc(ln_var, 1)
            else:
                dve.wait_ge(ln_pow, k + 1)

        def split_step(eng, ops, bb, which, m):
            if m:
                eng.wait_ge(split_chain, 5 * (2 * bb + which) + m)
            if m == 0:
                ops.tensor_tensor(rope, tcos[:, :], tsin[:, :], ALU.add).then_inc(split_chain, 1)
            elif m == 2:
                ops.tensor_tensor(rest[:, :], rope, parts[:, which, 0, :], ALU.subtract).then_inc(split_chain, 1)
            else:
                ops.tensor_tensor(parts[:, which, 2, :], rest[:, :], parts[:, which, 1, :], ALU.subtract
                                  ).then_inc(split_chain, 1)

        @block.sync
        def _(sp):
            xv = x.rearrange("b (t p) d -> p (b t) d", p=P)
            sp.dma_start(xall[:, 0:NT, :], xv[:, 0:NT, :]).then_inc(x_in, 16)
            for dst, src in ((wq, Wq), (wk, Wk), (wv, Wv), (wo, Wo), (cosT, cos), (sinT, sin)):
                sp.dma_start(dst[:, :], src).then_inc(w_in, 16)
            sp.dma_start(xall[:, NT:, :], xv[:, NT:, :]).then_inc(x_rest_in, 16)
            sp.dma_start(wr[:, :], Wr).then_inc(wr_in, 16)
            sp.dma_start(w1s[:, :, :], W1.rearrange("e h f -> h e f")).then_inc(we_in, 16)

            def store_parts(bb, which):
                sp.wait_ge(split_chain, 5 * (2 * bb + which + 1))
                dram = (q_dram, k_dram)[which]
                for at in range(dram.shape[2]):
                    sp.dma_start(dram[bb, :, at], parts[:, which, at % 3, :]).then_inc(parts_out, 16)

            def load_stack(bb, g):
                sp.wait_ge(parts_out, 128 * bb + 128)
                heads = slice(G * g, G * g + G)
                for r in range(3):
                    rows = slice(3 * DK * r, 3 * DK * (r + 1))
                    q_src = q_dram[bb, heads].rearrange("h n d s -> (n d) h s")
                    for half in range(2):
                        sp.dma_start(stq[g][rows, half, :, :],
                                     q_src[:, :, 512 * half:512 * half + 512]).then_inc(stack_in[g], 16)
                    sp.dma_start(stk[g][rows, :, :],
                                 k_dram[bb, heads, r:r + 3].rearrange("h n d s -> (n d) h s")).then_inc(stack_in[g], 16)

            def shift_rows(u, g, half):
                sp.wait_ge(mparts_done, 2 * u + half + 1)
                for part in range(3):
                    sp.dma_start(stq[g][SHIFT_AT + part:SHIFT_AT + part + 1, half, :, :],
                                 mparts[:, half, part, :]).then_inc(mrow_in[half], 16)

            for t in range(NTILES - 2 * T):
                if t == 0:
                    sp.wait_ge(consts, N_CONSTS)
                sp.dma_start(x_rows[E * REGION + P * t:E * REGION + P * (t + 1), :], blank[:, E + t, :]).then_inc(spare_in, 16)

            def section(b, steps):
                for kind, db, g, m, n in steps:
                    if kind == "SQ":
                        store_parts(b + db, m)
                    if kind == "SK":
                        if steps is before:
                            sp.wait_ge(zeroed[g], 2)
                        else:
                            sp.wait_ge(pv_done, 1 + NPV * (NG * b + g + 1))
                        load_stack(b + db, g)
                    if kind == "MT":
                        shift_rows(NG * (b + db) + g, g, m)
                    if kind == "W2":
                        sp.wait_ge(pv_done, 1 + NPV * (NG * b + 2))
                        sp.dma_start(w2s[:, :, :, :], W2.rearrange("e (c p) h -> p e c h", p=P)).then_inc(w2_in, 16)

            sections(sp, section)
            sp.wait_ge(table_done, N_TABLE)
            for e in range(E):
                row = sp.value_load(tinfo[0:1, 2, e:e + 1], min_val=REGION * e, max_val=REGION * e + T * P)
                sp.dma_start(x_rows[bass.ds(row, P), :], blank[:, e, :]).then_inc(tails_in, 16)

        @block.tensor
        def _(pe):
            pe.sem_inc(pv_done, 1)
            pe.wait_ge(ident_done, 2)
            pe.wait_ge(x_in, 16)

            def pv_group(b, steps, db, g, n, part):
                half, j = PV_GROUPS[n]
                u = NG * (b + db) + g
                w = width(half, j)
                first, last = (0, w) if PV_PARTS[n] == 1 else (w // 2, w) if part == 0 else (0, w // 2)
                if part == 0:
                    taken(pe, b, steps, "E", db, g, PV_LAST[n])
                if first == 0 and DIAGONAL[PV_LAST[n]]:
                    pe.wait_ge(masked, sum(DIAGONAL) * u + sum(DIAGONAL[:PV_LAST[n] + 1]))
                if j == 0 and part == 0:
                    if half == 0:
                        pe.wait_ge(vaug_done, u + 1)
                    pe.wait_ge(osb_done, 2 * u + 1 + half)
                for h in range(G):
                    k = next(k for k in range(NE) if GROUP_OF[k] == n and h in E_ITEMS[k][2])
                    bank, col = place(E_ITEMS[k][2], h, w)
                    mm = nc.tensor.matmul(opsum[half][32 * h:32 * h + 32, 512 - w + first:512 - w + last],
                                          vaug[g][:, j, h, :], probs[k % RING][:, bank, col + first:col + last],
                                          start=(j == 0), stop=(j == 4 * half + 3), skip_group_check=True)
                if part + 1 == PV_PARTS[n]:
                    mm.then_inc(pv_done, 1)

            def fill(b, steps, kind, db, g, m, n):
                s, used = slot_of(b, n)
                ps = slot[s]
                if not (steps is before and n < SLOTS):
                    pe.wait_ge(left[s], used)
                at = lambda t: ps[:, t // 4, P * (t % 4):P * (t % 4) + P]
                if kind == "P" and m == 0:
                    for t in range(NT):
                        src = xall[:, t, :] if steps is before else xnext[:, t, :]
                        if steps is not before and t == 0:
                            pe.wait_ge(xnext_done, b + 1)
                        mm = nc.tensor.transpose(at(t), src, ident[:, :])
                elif kind == "P":
                    if m == 1:
                        taken(pe, b, steps, "P", 1, 0, 0)
                        pe.wait_ge(w_in, 96)
                        pe.wait_ge(wrot, 4)
                    if m < 5:
                        w = (wq, wqr, wk, wkr)[m - 1]
                        for c in range(2):
                            mm = nc.tensor.matmul(ps[:, c, :], w[:, :], xT[:, 512 * c:512 * c + 512],
                                                  start=True, stop=True)
                    else:
                        for t in range(NT):
                            mm = nc.tensor.matmul(at(t), xT[:, P * t:P * t + P], wv[:, :], start=True, stop=True,
                                                  skip_group_check=True)
                elif kind == "M":
                    half, i, heads = M_ITEMS[m]
                    if m == 0:
                        pe.wait_ge(stack_in[g], 16 * 9 * (b + db + 1))
                        if steps is before and g == 0:
                            pe.wait_ge(consts, N_CONSTS)
                    keys = P * (i + 1)
                    for h in heads:
                        for c in range(0, keys, 512):
                            w = min(512, keys - c)
                            bank, col = (c // 512, 0) if len(heads) == 1 else place(heads, h, keys)
                            diag = c + w == keys
                            mm = nc.tensor.matmul(ps[:, bank, col:col + w], stq[g][0:SHIFT_AT, half, h, P * (i % 4):P * (i % 4) + P],
                                                  stk[g][0:SHIFT_AT, h, c:c + w], start=True, stop=not diag,
                                                  skip_group_check=True)
                            if diag:
                                mm = nc.tensor.matmul(ps[:, bank, col + w - P:col + w], identb[:, :], maskb[:, :],
                                                      start=False, stop=True, skip_group_check=True)
                elif kind == "MT":
                    taken(pe, b, steps, "M", db, g, NM - 1 if m else M_HALF - 1)
                    mm = nc.tensor.transpose(ps[0:16, 0, 0:P], negm[:, g % 2, m, :], ident[:, :])
                elif kind == "E":
                    half, j, heads = E_ITEMS[m]
                    if m in (0, E_HALF):
                        pe.wait_ge(mrow_in[half], 48 * (NG * (b + db) + g + 1))
                    w = width(half, j)
                    for h in heads:
                        bank, col = place(heads, h, w)
                        mm = nc.tensor.matmul(ps[:, bank, col:col + w], stk[g][:, h, P * j:P * j + P],
                                              stq[g][:, half, h, 512 - w:512],
                                              start=True, stop=True, skip_group_check=True)
                elif kind == "N":
                    pe.wait_ge(osb_done, 2 + 2 * (NG * (b + db) + g) + m + 1)
                    for t in range(4):
                        mm = nc.tensor.transpose(ps[:, 0, P * t:P * t + P], osb[:, m, P * t:P * t + P], ident[:, :])
                elif kind == "AT":
                    taken(pe, b, steps, "N", 0, NG - 1, 1)
                    for t in range(NT):
                        mm = nc.tensor.transpose(at(t), attn[:, t, :], ident[:, :])
                elif kind == "XT":
                    pe.wait_ge(x1_done, b + 1)
                    for t in range(NT):
                        mm = nc.tensor.transpose(at(t), x1[0][:, t, 0:D], ident[:, :])
                elif kind == "LG":
                    taken(pe, b, steps, "XT", 0, 0, 0)
                    pe.wait_ge(wr_in, 16)
                    for t in range(NT):
                        mm = nc.tensor.matmul(ps[:, 0, E * t:E * t + E], attnT[:, P * t:P * t + P], wr[:, :],
                                              start=True, stop=True, skip_group_check=True)
                elif kind == "CT":
                    pe.wait_ge(rt_chain, RT * b + RT_CNT)
                    for c, w in enumerate((before_b, onesb)):
                        mm = nc.tensor.matmul(ps[:, 0, NT * E * c:NT * E * (c + 1)], w[:, :],
                                              cntb[:, :, :].rearrange("p t e -> p (t e)"), start=True, stop=True,
                                              skip_group_check=True)
                elif kind == "O":
                    taken(pe, b, steps, "AT", 0, 0, 0)
                    for t in range(NT):
                        mm = nc.tensor.matmul(at(t), attnT[:, P * t:P * t + P], wo[:, :], start=True, stop=True,
                                              skip_group_check=True)
                if kind == "D":
                    pe.sem_inc(filled[s], 1)
                else:
                    mm.then_inc(filled[s], 1)

            def section(b, steps):
                waiting = []
                for kind, db, g, m, n in steps:
                    if kind == "C":
                        while waiting and waiting[0] < (db, g, NPV if m else 4):
                            pv_group(b, steps, *waiting.pop(0))
                    if kind not in IN_SLOT:
                        continue
                    if kind == "E":
                        while waiting:
                            wdb, wg, group, part = waiting[0]
                            item = PV_LAST[group]
                            late = part == 1 or DIAGONAL[item] and PV_PARTS[group] == 1
                            if NE * (NG * (db - wdb) + g - wg) + m - item < 2 + late:
                                break
                            pv_group(b, steps, *waiting.pop(0))
                    fill(b, steps, kind, db, g, m, n)
                    if kind == "E":
                        if m in PV_LAST:
                            group = PV_LAST.index(m)
                            waiting += [(db, g, group, part) for part in range(PV_PARTS[group])]
                for group in waiting:
                    pv_group(b, steps, *group)

            sections(pe, section)

        @block.scalar
        def _(act):
            act.sem_inc(osb_done, 2)

            def section(b, steps):
                for kind, db, g, m, n in steps:
                    s, used = slot_of(b, n)
                    flat = slot[s][:, :, :].rearrange("p a c -> p (a c)")
                    if kind == "P" and m == 0:
                        act.wait_ge(filled[s], used + 1)
                        nc.scalar.activation(xT[:, :], flat, ACT.Copy).then_inc(left[s], 1)
                    if kind == "P" and m == 5:
                        act.wait_ge(filled[s], used + 1)
                        if steps is not before:
                            act.wait_ge(vaug_done, NG * (b + 1))
                        nc.scalar.activation(vraw[:, :, :].rearrange("p a c -> p (a c)"), flat,
                                             ACT.Copy).then_inc(left[s], 1)
                    if kind == "E":
                        half, j, heads = E_ITEMS[m]
                        if not (steps is before and g == 0 and m < RING):
                            e = m - RING
                            act.wait_ge(pv_done, 2 + NPV * (NG * (b + db) + g + e // NE) + GROUP_OF[e % NE])
                        act.wait_ge(filled[s], used + 1)
                        wide = width(half, j) * len(heads) // 2
                        nc.scalar.activation(probs[m % RING][:, :, 0:wide], slot[s][:, :, 0:wide], ACT.Exp,
                                             scale=SCALE).then_inc(left[s], 1)
                    if kind == "C":
                        act.wait_ge(pv_done, 1 + NPV * (NG * (b + db) + g) + (NPV if m else 4))
                        nc.scalar.activation(osb[:, m, :], opsum[m][:, :], ACT.Copy).then_inc(osb_done, 1)
                    if kind == "G" and m in (1, 3):
                        act.wait_ge(split_chain, 5 * (2 * (b + db) + g) + m)
                        nc.scalar.activation(parts[:, g, m // 2, :], rope if m == 1 else rest[:, :],
                                             ACT.Copy).then_inc(split_chain, 1)
                    if kind == "R" and m == 2:
                        act.wait_ge(rt_chain, RT * b + 2)
                        nc.scalar.activation(rt[1][:, :, :], rt[0][:, :, :], ACT.Exp).then_inc(rt_exp, 1)
                    if kind == "XT":
                        act.wait_ge(x1_done, b + 1)
                        nc.scalar.activation(x1[1][:, :, 0:D], x1[0][:, :, 0:D], ACT.Copy).then_inc(x1_twin, 1)
                    if kind in ("AT", "XT"):
                        act.wait_ge(filled[s], used + 1)
                        nc.scalar.activation(attnT[:, :], flat, ACT.Copy).then_inc(left[s], 1)

            sections(act, section)

        @block.vector
        def _(dve):
            two_ones = float(np.array([0x3F803F80], np.uint32).view(np.float32)[0])
            keys = [stk[g].rearrange("p h k -> p (h k)").bitcast(F32) for g in range(NG)]

            def stack_keys(g):
                nc.vector.memset(keys[g], 0.0).then_inc(keys_zeroed, 1)
                dve.wait_ge(keys_zeroed, g + 1)
                nc.vector.memset(keys[g][SHIFT_AT:SHIFT_AT + 3, :], two_ones).then_inc(zeroed[g], 1)

            stack_keys(0)
            dve.wait_ge(w_in, 96)
            for w, r in ((wq, wqr), (wk, wkr)):
                pair = w[:, :].rearrange("p (c two) -> p c two", two=2)
                rot = r[:, :].rearrange("p (c two) -> p c two", two=2)
                nc.vector.tensor_scalar(rot[:, :, 0], pair[:, :, 1], -1.0, None, ALU.mult).then_inc(wrot, 1)
                nc.vector.tensor_copy(rot[:, :, 1], pair[:, :, 0]).then_inc(wrot, 1)

            def section(b, steps):
                for kind, db, g, m, n in steps:
                    s, used = slot_of(b, n)
                    ps = slot[s]
                    flat = ps[:, :, :].rearrange("p a c -> p (a c)")
                    if kind == "P" and 1 <= m < 5:
                        dve.wait_ge(filled[s], used + 1)
                        if m in (1, 3) and not (steps is before and m == 1):
                            which = (m - 3) // 2
                            dve.wait_ge(split_chain, 5 * (2 * (b + db) + which) + 1)
                        if m % 2:
                            nc.vector.tensor_tensor(tcos[:, :], flat, cosT[:, :], ALU.mult).then_inc(left[s], 1)
                        else:
                            nc.vector.tensor_tensor(tsin[:, :], flat, sinT[:, :], ALU.mult).then_inc(left[s], 1)
                    if kind == "SQ" and steps is before and m == 1:
                        for unit in range(1, NG):
                            stack_keys(unit)
                    if kind == "G" and m % 2 == 0 and steps is before:
                        if m == 0:
                            taken(dve, b, steps, "P", 1, 0, 2 * g + 1)
                            taken(dve, b, steps, "P", 1, 0, 2 * g + 2)
                        split_step(dve, nc.vector, b + db, g, m)
                    if kind == "M":
                        half, i, heads = M_ITEMS[m]
                        dve.wait_ge(filled[s], used + 1)
                        keys = P * (i + 1)
                        out_ = negm[:, g % 2, half, :].rearrange("p (j a q) -> p a j q", a=2, j=2)
                        q = i % 4
                        if len(heads) == G:
                            src = ps[:, :, 0:2 * keys].rearrange("p a (j k) -> p a j k", j=2)
                            dst = out_[:, :, :, q]
                        elif len(heads) == 2:
                            src = ps[:, :, 0:keys]
                            dst = out_[:, :, heads[0] // 2, q]
                        else:
                            src = flat[:, 0:keys]
                            dst = out_[:, heads[0] % 2, heads[0] // 2, q:q + 1]
                        nc.vector.tensor_reduce(dst, src, AX.X, ALU.max, negate=True).then_inc(left[s], 1)
                    if kind == "MT":
                        dve.wait_ge(filled[s], used + 1)
                        if not (steps is before and g == 0):
                            dve.wait_ge(mparts_done, 2 * (NG * (b + db) + g - 1) + m + 1)
                        nc.vector.tensor_copy(mrow[:, m, :], ps[0:16, 0, 0:P]).then_inc(left[s], 1)
                    if kind == "N":
                        u = NG * (b + db) + g
                        dve.wait_ge(filled[s], used + 1)
                        view = ps[:, 0, :].rearrange("p (t h c) -> p t h c", t=4, h=G)
                        nc.vector.reciprocal(rsum[:, m, :, :], view[:, :, :, DK]).then_inc(dve_recip, 1)
                        dve.wait_ge(dve_recip, 2 * u + m + 1)
                        nc.vector.tensor_tensor(
                            attn[:, 4 * m:4 * m + 4, G * DK * g:G * DK * (g + 1)].rearrange("p t (h c) -> p t h c", h=G),
                            view[:, :, :, 0:DK], rsum[:, m, :, :].unsqueeze(3).to_broadcast([P, 4, G, DK]),
                            ALU.mult).then_inc(left[s], 1)
                    if kind == "O":
                        dve.wait_ge(filled[s], used + 1)
                        nc.vector.tensor_tensor(res, ps[:, :, :].rearrange("p a (c d) -> p (a c) d", d=D),
                                                xall[:, tokens(b), :], ALU.add).then_inc(left[s], 1)
                    if kind == "L":
                        if m == 0:
                            taken(dve, b, steps, "O", 0, 0, 0)
                        layer_norm(dve, b, res, sq, m)
                        if m == LN_STEPS - 1:
                            dve.wait_ge(x1_free, b + 1)
                            nc.vector.tensor_tensor(x1[0][:, :, 0:D], res, bc(stat[:, 3, :]), ALU.mult).then_inc(x1_done, 1)
                    if kind == "LG":
                        dve.wait_ge(filled[s], used + 1)
                        nc.vector.tensor_copy(rt[0][:, :, :].rearrange("p t e -> p (t e)"), ps[:, 0, 0:NT * E]
                                              ).then_inc(left[s], 1)
                    if kind == "R":
                        if m == 0:
                            taken(dve, b, steps, "LG", 0, 0, 0)
                        choose(b, m)
                        if m == 0:
                            dve.wait_ge(x1_done, b + 1)
                            settled()
                            nc.vector.tensor_copy(xall[:, tokens(b), :], x1[0][:, :, 0:D]).then_inc(x1_kept, 1)
                    if kind == "CT":
                        dve.wait_ge(filled[s], used + 1)
                        nc.vector.tensor_copy(before_it[:, :, :, :].rearrange("p w t e -> p (w t e)"),
                                              ps[:, 0, 0:2 * NT * E]).then_inc(left[s], 1)
                    if kind == "K":
                        if m == 0:
                            taken(dve, b, steps, "CT", 0, 0, 0)
                        rank(b, m)
                    if kind == "X":
                        dve.wait_ge(x_rest_in, 16)
                        dve.wait_ge(vaug_done, NG * (b + 1))
                        settled()
                        nc.vector.tensor_copy(xnext[:, :, :], xall[:, tokens(b + 1), :]).then_inc(xnext_done, 1)
                    if kind == "D":
                        dve.wait_ge(filled[s], used + 1)
                        dve.sem_inc(left[s], 1)

            def settled():
                dve.sem_inc(dve_settled, 1)

            def over_experts(s_):
                return s_.unsqueeze(2).to_broadcast([P, s_.shape[1], E])

            def over_tiles(s_):
                return s_.unsqueeze(1).to_broadcast([P, NT, E])

            def choose(b, m):
                v = nc.vector
                cut, ex, g, cand, tmp = (x[:, :, :] for x in rt)
                if m:
                    dve.wait_ge(rt_chain, RT * b + m)
                if m == 0:
                    ins = v.tensor_reduce(rs[:, 0, :], cut, AX.X, ALU.max)
                elif m == 1:
                    ins = v.tensor_tensor(cut, cut, over_experts(rs[:, 0, :]), ALU.subtract)
                elif m == 2:
                    dve.wait_ge(rt_exp, b + 1)
                    ins = v.tensor_reduce(rs[:, 1, :], ex, AX.X, ALU.add)
                elif m == 3:
                    ins = v.reciprocal(rs[:, 2, :], rs[:, 1, :])
                elif m == 4:
                    ins = v.tensor_tensor(g, ex, over_experts(rs[:, 2, :]), ALU.mult)
                elif m in (5, 11):
                    ins = v.tensor_reduce(rs[:, m // 11, :], g, AX.X, ALU.max)
                elif m in (6, 12):
                    ins = v.tensor_tensor(tmp, g, over_experts(rs[:, m // 12, :]), ALU.is_equal)
                elif m in (7, 13):
                    ins = v.tensor_tensor(cand, tmp, over_tiles(rev[:, :]), ALU.mult)
                elif m in (8, 14):
                    ins = v.tensor_reduce(rs[:, 3, :], cand, AX.X, ALU.max)
                elif m in (9, 15):
                    ins = v.tensor_tensor(cut if m == 9 else tmp, over_tiles(rev[:, :]), over_experts(rs[:, 3, :]),
                                          ALU.is_equal)
                elif m == 10:
                    ins = v.scalar_tensor_tensor(g, cut, -2.0, g, ALU.mult, ALU.add)
                elif m == 16:
                    ins = v.tensor_tensor(cntb[:, :, :], cut, tmp, ALU.add)
                elif m in (17, 18):
                    ins = v.tensor_copy(x1[m - 17][:, :, D].bitcast(U32), y_of[:, m - 17, :])
                elif m == 19:
                    ins = v.tensor_scalar(y_of[:, :, :], y_of[:, :, :], float(NT * P), None, ALU.add)
                elif m == 20:
                    ins = v.tensor_tensor(rs[:, 2, :], rs[:, 0, :], rs[:, 1, :], ALU.add)
                elif m == 21:
                    ins = v.reciprocal(rs[:, 3, :], rs[:, 2, :])
                else:
                    ins = v.tensor_tensor(x1[m - 22][:, :, D + 1], rs[:, m - 22, :], rs[:, 3, :], ALU.mult)
                ins.then_inc(rt_chain, 1)

            def rank(b, m):
                v = nc.vector
                cut, ex, g, cand, tmp = (x[:, :, :] for x in rt)
                dve.wait_ge(rt_chain, RT * b + CHOICE_STEPS + m)
                if m < NT:
                    ins = v.tensor_tensor(run[:, m + 1, :], run[:, m, :], before_it[:, 1, m, :], ALU.add)
                elif m == 8:
                    ins = v.tensor_tensor(g, before_it[:, 0], run[:, 0:NT, :], ALU.add)
                elif m == 9:
                    ins = v.tensor_copy(run[:, 0, :], run[:, NT, :])
                elif m == 10:
                    ins = v.tensor_tensor(cand, g, over_tiles(first_rows[:, :]), ALU.add)
                elif m == 11:
                    ins = v.tensor_tensor(ex, cand, cut, ALU.mult)
                elif m == 12:
                    ins = v.tensor_tensor(g, cand, tmp, ALU.mult)
                elif m in (13, 14):
                    ins = v.tensor_reduce(row_f[:, m - 13, :], ex if m == 13 else g, AX.X, ALU.add)
                else:
                    ins = v.tensor_copy(xr[:, :, :], row_f[:, :, :])
                ins.then_inc(rt_chain, 1)

            def tables(dve):
                v = nc.vector
                done = [0]

                def step(ins):
                    done[0] += 1
                    ins.then_inc(table_done, 1)
                    dve.wait_ge(table_done, done[0])
                n_e = run[:, 0, :]
                share = tbl[:, 0, 0:E]
                n_tiles = tbl[:, 1, 0:E]
                end = tbl[:, 2, 0:E + 1]
                shift = tbl[:, 3, 0:E]
                is_over = tsin[:, 0:NTILES * E].rearrange("p (t e) -> p t e", e=E)
                over_tiles_of = sinT[:, 0:NTILES * E].rearrange("p (t e) -> p t e", e=E)
                begun = tsin[:, 0:E * T].rearrange("p (e t) -> p e t", e=E)
                wide = lambda s_, n: s_.unsqueeze(1).to_broadcast([P, n, s_.shape[1]])
                deep = lambda s_, n: s_.unsqueeze(2).to_broadcast([P, s_.shape[1], n])
                step(v.tensor_scalar(share, n_e, 1.0 / P, None, ALU.mult))
                step(v.tensor_tensor(begun, deep(share, T), wide(tile_no[:, 0:T], E), ALU.is_gt))
                step(v.tensor_reduce(n_tiles, begun, AX.X, ALU.add))
                step(v.memset(end[:, 0:1], 0.0))
                for e in range(E):
                    step(v.tensor_tensor(end[:, e + 1:e + 2], end[:, e:e + 1], n_tiles[:, e:e + 1], ALU.add))
                step(v.scalar_tensor_tensor(shift, end[:, 0:E], float(P), first_rows[:, :], ALU.mult, ALU.subtract))
                step(v.tensor_tensor(is_over, deep(tile_no[:, :], E), wide(end[:, 1:E + 1], NTILES), ALU.is_ge))
                expert, tiles_over, row = (tbl[:, i, 0:NTILES] for i in (6, 7, 4))
                step(v.tensor_reduce(expert, is_over, AX.X, ALU.add))
                step(v.tensor_tensor(over_tiles_of, is_over, wide(n_tiles, NTILES), ALU.mult))
                step(v.tensor_reduce(tiles_over, over_tiles_of, AX.X, ALU.add))
                step(v.tensor_tensor(row, tile_no[:, :], tiles_over, ALU.subtract))
                step(v.tensor_scalar(tiles_over, expert, float(REGION), None, ALU.mult))
                step(v.scalar_tensor_tensor(row, row, float(P), tiles_over, ALU.mult, ALU.add))
                step(v.tensor_copy(tinfo[:, 1, :], row))
                step(v.tensor_scalar(expert, expert, float(E - 1), None, ALU.min))
                step(v.tensor_copy(tinfo[:, 0, :], expert))
                step(v.tensor_tensor(shift, first_rows[:, :], n_e, ALU.add))
                step(v.tensor_copy(tinfo[:, 2, 0:E], shift))

            nc.vector.memset(run[:, 0, :], 0.0).then_inc(run_zero, 1)
            dve.wait_ge(run_zero, 1)
            sections(dve, section)
            dve.wait_ge(rt_chain, RT * B)
            dve.wait_ge(x1_kept, B)
            tables(dve)

        @block.gpsimd
        def _(pool):
            pool.sem_inc(x1_free, 1)
            nc.gpsimd.memset(ident[:, :], 0.0).then_inc(ident_done, 1)
            pool.wait_ge(ident_done, 1)
            nc.gpsimd.affine_select(out=ident[:, :], in_=ident[:, :], compare_op=ALU.not_equal, fill=1.0, base=0,
                                    pattern=[[-1, P]], channel_multiplier=1).then_inc(ident_done, 1)
            for g in range(NG):
                nc.gpsimd.memset(stq[g][:, :, :, :].rearrange("p a h q -> p (a h q)").bitcast(F32), 0.0
                                 ).then_inc(zeroed[g], 1)

            nc.gpsimd.memset(maskb[:, :], 0.0).then_inc(consts, 1)
            pool.wait_ge(consts, 1)
            nc.gpsimd.affine_select(out=maskb[:, :], in_=maskb[:, :], compare_op=ALU.is_ge, fill=NEG, base=0,
                                    pattern=[[-1, P]], channel_multiplier=1).then_inc(consts, 1)
            pool.wait_ge(ident_done, 2)
            nc.gpsimd.tensor_copy(identb[:, :], ident[:, :]).then_inc(consts, 1)
            nc.gpsimd.memset(neg_half[:, :], -0.5).then_inc(consts, 1)
            nc.gpsimd.memset(blank[:, :, :], 0.0).then_inc(consts, 1)
            nc.gpsimd.memset(onesb[:, :], 1.0).then_inc(consts, 1)
            nc.gpsimd.memset(before_b[:, :], 1.0).then_inc(consts, 1)
            nc.gpsimd.iota(counts[:, :], [[1, NTILES]], base=0, channel_multiplier=0).then_inc(consts, 1)
            nc.gpsimd.iota(y_row[:, :, :], [[T * P, 2], [P, NT]], base=0, channel_multiplier=1).then_inc(consts, 1)
            pool.wait_ge(consts, 9)
            nc.gpsimd.iota(blank[:, :, D].bitcast(U32), [[P, NTILES - 2 * T + E]], base=2 * T * P,
                           channel_multiplier=1).then_inc(consts, 1)
            nc.gpsimd.affine_select(out=before_b[:, :], in_=before_b[:, :], compare_op=ALU.is_gt, fill=0.0, base=0,
                                    pattern=[[1, P]], channel_multiplier=-1).then_inc(consts, 1)
            nc.gpsimd.tensor_copy(tile_no[:, :], counts[:, :]).then_inc(consts, 1)
            nc.gpsimd.tensor_copy(y_of[:, :, :], y_row[:, :, :]).then_inc(consts, 1)
            pool.wait_ge(consts, 13)
            nc.gpsimd.tensor_scalar(first_rows[:, :], tile_no[:, 0:E], float(REGION), 0.0, ALU.mult, ALU.add
                                    ).then_inc(consts, 1)
            nc.gpsimd.tensor_scalar(rev[:, :], tile_no[:, 0:E], -1.0, float(E), ALU.mult, ALU.add
                                    ).then_inc(consts, 1)
            nc.gpsimd.memset(tinfo[:, :, :], 0).then_inc(consts, 1)
            for g in range(NG):
                nc.gpsimd.memset(vaug[g][:, :, :, :], 0.0).then_inc(consts, 1)
            pool.wait_ge(consts, 16 + NG)
            for g in range(NG):
                nc.gpsimd.memset(vaug[g][:, :, :, DK:DK + 1], 1.0).then_inc(consts, 1)
            pool.wait_ge(consts, N_CONSTS)

            def settled():
                pool.sem_inc(pool_settled, 1)

            def lay_v(g):
                settled()
                nc.gpsimd.tensor_copy(vaug[g][:, :, :, 0:DK],
                                      vraw[:, :, G * DK * g:G * DK * (g + 1)].rearrange("p t (h c) -> p t h c", h=G)
                                      ).then_inc(vaug_done, 1)

            def split_max(u, first, m):
                if not first:
                    pool.wait_ge(mrow_in[m], 48 * u)
                k = 3 * (2 * u + m)
                a, r, p = mrow[:, m, :], mrest[:, m, :], mparts[:, m]
                settled()
                nc.gpsimd.tensor_copy(p[:, 0, :], a).then_inc(max_chain, 1)
                pool.wait_ge(max_chain, k + 1)
                nc.gpsimd.tensor_tensor(r, a, p[:, 0, :], ALU.subtract).then_inc(max_chain, 1)
                nc.gpsimd.tensor_tensor(p[:, 1, :], a, p[:, 0, :], ALU.subtract).then_inc(max_chain, 1)
                pool.wait_ge(max_chain, k + 3)
                nc.gpsimd.tensor_tensor(p[:, 2, :], r, p[:, 1, :], ALU.subtract).then_inc(mparts_done, 1)

            def section(b, steps):
                for kind, db, g, m, n in steps:
                    if kind == "G" and m % 2 == 0 and steps is not before:
                        if m == 0:
                            taken(pool, b, steps, "P", 1, 0, 2 * g + 2)
                            pool.wait_ge(parts_out, 128 * (b + db))
                        split_step(pool, nc.gpsimd, b + db, g, m)
                    if kind == "V":
                        if (steps is before or steps is body) and g == 0:
                            taken(pool, b, steps, "P", 1, 0, 5)
                        if steps is not before:
                            pool.wait_ge(pv_done, 1 + NPV * (NG * b + g + 1))
                        lay_v(g)
                    if kind == "MT":
                        taken(pool, b, steps, "MT", db, g, m)
                        split_max(NG * (b + db) + g, steps is before and g == 0, m)
                    if kind == "E" and DIAGONAL[m]:
                        half, j, heads = E_ITEMS[m]
                        taken(pool, b, steps, "E", db, g, m)
                        w = width(half, j)
                        if len(heads) == G:
                            v = probs[m % RING][:, :, 0:2 * w].rearrange("p a (j q) -> p a j q", j=2)[:, :, :, 0:P]
                            pattern = [[0, 2], [0, 2], [1, P]]
                        else:
                            v = probs[m % RING][:, :, 0:P]
                            pattern = [[0, 2], [1, P]]
                        settled()
                        nc.gpsimd.affine_select(out=v, in_=v, compare_op=ALU.is_ge, fill=0.0, base=0,
                                                pattern=pattern, channel_multiplier=-1).then_inc(masked, 1)
                    if kind == "L" and m == 3:
                        norm_squares(pool, b, res, sq)
                    if kind == "L" and m == 5:
                        norm_power(pool, b)
                    if kind == "S":
                        if m == 0:
                            pool.wait_ge(rt_chain, RT * b + RT)
                            settled()
                            pool.wait_ge(x1_twin, b + 1)
                            settled()
                        t, k = m // 2, m % 2
                        nc.gpsimd.indirect_dma_start(
                            x_rows, bass.IndirectOffsetOnAxis(ap=xr[:, k, t:t + 1], axis=0), x1[k][:, t, :], None
                        ).then_inc(scattered, 16)
                    if kind == "F":
                        pool.wait_ge(scattered, 16 * 2 * NT * (b + 1))
                        pool.sem_inc(x1_free, 1)

            sections(pool, section)
        phase.close()
        attention.close()

        experts = ctx.enter_context(ExitStack())

        def sb(name, shape, dt=F32):
            return experts.enter_context(nc.sbuf_tensor(name, shape, dt))

        XB, SB = 8, 4
        xin = [sb(f"xin{i}", [P, DW]) for i in range(XB)]
        xinT = [sb(f"xinT{i}", [P, P]) for i in range(SB)]
        hid = [sb(f"hid{i}", [P, F]) for i in range(SB)]
        w1e = [sb(f"w1e{i}", [P, F]) for i in range(SB)]
        y = [sb(f"y{i}", [P, D]) for i in range(SB)]
        yk = [sb(f"yk{b}", [P, 2, NT, D]) for b in range(B)]
        stats = sb("stats", [P, B, 4, NT])
        x_ps = [opsum[i][:, 0:P] for i in range(2)]
        hid_ps = [slot[i // 2][:, i % 2, :] for i in range(SB)]
        y_ps = [slot[2][:, i, 0:D] for i in range(2)]

        tile_in = [sem(f"tile_in{i}") for i in range(XB)]
        x_turned = sem("x_turned")
        xT_out = sem("xT_out")
        w1_there = sem("w1_there")
        hid_made = sem("hid_made")
        hid_out = sem("hid_out")
        y_made = sem("y_made")
        y_out = sem("y_out")
        y_stored = [sem(f"y_stored{i}") for i in range(SB)]
        yk_in = [sem(f"yk_in{b}") for b in range(B)]
        summed = sem("summed")
        mixed = sem("mixed")
        squared = sem("squared")
        sq_summed = sem("sq_summed")
        out_ready = sem("out_ready")
        out_stored = sem("out_stored")

        phase = ctx.enter_context(ExitStack())
        block = phase.enter_context(nc.Block())

        def tile_loop(eng, step, last):
            assert NTILES % XB == 0 and XB % SB == 0
            for k in range(XB):
                step(k, k % XB, k // XB)
            with eng.Fori(1, NTILES // XB) as i:
                for u in range(XB):
                    step(XB * i + u, u, i)
            for k in range(NTILES, NTILES + last):
                step(k, k % XB, k // XB)

        def there(k):
            return not isinstance(k, int) or 0 <= k < NTILES

        def after_first(k, n):
            return not isinstance(k, int) or k >= n

        @block.sync
        def _(sp):
            sp.wait_ge(scattered, 16 * 2 * T)
            sp.wait_ge(tails_in, 16 * E)
            sp.wait_ge(spare_in, 16 * (NTILES - 2 * T))

            def step(k, u, r):
                row = sp.value_load(tinfo[0:1, 1, bass.ds(k, 1)], min_val=0, max_val=(E + 1) * REGION - P)
                if after_first(k, XB):
                    sp.wait_ge(y_stored[u % SB], 16 * (XB // SB * (r - 1) + u // SB + 1))
                sp.dma_start(xin[u][:, :], x_rows[bass.ds(row, P), :]).then_inc(tile_in[u], 16)

            tile_loop(sp, step, 0)
            for i in range(SB):
                sp.wait_ge(y_stored[i], 16 * NTILES // SB)
            for b in range(B):
                for k in range(2):
                    at = (k * T + b * NT) * P
                    sp.dma_start(yk[b][:, k], y_rows[at:at + NT * P].rearrange("(t p) d -> p t d", p=P)
                                 ).then_inc(yk_in[b], 16)
            for b in range(B):
                sp.wait_ge(out_ready, b + 1)
                sp.dma_start(out[b].rearrange("(t p) d -> p t d", p=P), yk[b][:, 1]).then_inc(out_stored, 16)
            sp.wait_ge(out_stored, 16 * B)

        @block.tensor
        def _(pe):
            pe.wait_ge(w2_in, 16)

            def expert(k):
                return pe.value_load(tinfo[0:1, 0, bass.ds(k, 1)], min_val=0, max_val=E - 1)

            def turn_x(k, u, r):
                pe.wait_ge(tile_in[u], 16 * (r + 1))
                if after_first(k, 2):
                    pe.wait_ge(xT_out, k - 1)
                nc.tensor.transpose(x_ps[u % 2], xin[u][:, 0:D], ident[:, :]).then_inc(x_turned, 1)

            def first(k, u):
                pe.wait_ge(xT_out, k + 1)
                pe.wait_ge(w1_there, k + 1)
                if after_first(k, SB):
                    pe.wait_ge(hid_out, k - SB + 1)
                for c in range(FC):
                    mm = nc.tensor.matmul(hid_ps[u % SB][:, P * c:P * c + P], w1e[u % SB][:, P * c:P * c + P],
                                          xinT[u % SB][:, :], start=True, stop=True, skip_group_check=True)
                mm.then_inc(hid_made, 1)

            def second(k, u):
                e = expert(k)
                pe.wait_ge(hid_out, k + 1)
                if after_first(k, 2):
                    pe.wait_ge(y_out, k - 1)
                for c in range(FC):
                    mm = nc.tensor.matmul(y_ps[u % 2], hid[u % SB][:, P * c:P * c + P], w2s[:, bass.ds(e, 1), c, :],
                                          start=(c == 0), stop=(c == FC - 1))
                mm.then_inc(y_made, 1)

            def step(k, u, r):
                if there(k):
                    turn_x(k, u, r)
                if there(k - 1):
                    first(k - 1, (u - 1) % XB)
                if there(k - 2):
                    second(k - 2, (u - 2) % XB)

            tile_loop(pe, step, 2)

        @block.scalar
        def _(act):
            act.wait_ge(we_in, 16)

            def step(k, u, r):
                if there(k):
                    e = act.value_load(tinfo[0:1, 0, bass.ds(k, 1)], min_val=0, max_val=E - 1)
                    if after_first(k, SB):
                        act.wait_ge(hid_made, k - SB + 1)
                        act.sem_inc(act_settled, 1)
                    nc.scalar.activation(w1e[u % SB][:, :], w1s[:, bass.ds(e, 1), :].rearrange("p e f -> p (e f)"),
                                         ACT.Copy).then_inc(w1_there, 1)
                if there(k - 2):
                    act.wait_ge(hid_made, k - 1)
                    nc.scalar.activation(hid[(u - 2) % SB][:, :], hid_ps[(u - 2) % SB], ACT.Relu).then_inc(hid_out, 1)

            tile_loop(act, step, 2)
            for b in range(B):
                act.wait_ge(mixed, 4 * b + 4)
                nc.scalar.activation(yk[b][:, 0], yk[b][:, 1], ACT.Square).then_inc(squared, 1)

        @block.vector
        def _(dve):
            def step(k, u, r):
                if there(k):
                    dve.wait_ge(x_turned, k + 1)
                    nc.vector.tensor_copy(xinT[u % SB][:, :], x_ps[u % 2]).then_inc(xT_out, 1)
                if there(k - 2):
                    v = (u - 2) % XB
                    dve.wait_ge(y_made, k - 1)
                    if after_first(k - 2, SB):
                        stored = XB // SB * (r - (u < 2)) + v // SB
                        dve.wait_ge(y_stored[v % SB], 16 * stored)
                    nc.vector.tensor_scalar(y[v % SB][:, :], y_ps[v % 2], xin[v][:, D + 1:D + 2], None, ALU.mult
                                            ).then_inc(y_out, 1)

            tile_loop(dve, step, 2)

            v = nc.vector
            for i in range(B + 2):
                if i < B:
                    total = yk[i][:, 1]
                    dve.wait_ge(summed, i + 1)
                    v.tensor_tensor(total, total, yk[i][:, 0], ALU.add).then_inc(mixed, 1)
                    dve.wait_ge(mixed, 4 * i + 1)
                    v.tensor_reduce(stats[:, i, 0, :], total, AX.X, ALU.add).then_inc(mixed, 1)
                    dve.wait_ge(mixed, 4 * i + 2)
                    v.tensor_scalar(stats[:, i, 1, :], stats[:, i, 0, :], 1.0 / D, None, ALU.mult).then_inc(mixed, 1)
                    dve.wait_ge(mixed, 4 * i + 3)
                    v.tensor_tensor(total, total, bc(stats[:, i, 1, :]), ALU.subtract).then_inc(mixed, 1)
                if 1 <= i <= B:
                    dve.wait_ge(squared, i)
                    v.tensor_reduce(stats[:, i - 1, 2, :], yk[i - 1][:, 0], AX.X, ALU.add).then_inc(sq_summed, 1)
                    dve.wait_ge(sq_summed, i)
                    v.tensor_scalar(stats[:, i - 1, 0, :], stats[:, i - 1, 2, :], 1.0 / D, EPS, ALU.mult, ALU.add
                                    ).then_inc(ln_var, 1)
                if i >= 2:
                    total = yk[i - 2][:, 1]
                    dve.wait_ge(ln_pow, B + i - 1)
                    v.tensor_tensor(total, total, bc(stats[:, i - 2, 3, :]), ALU.mult).then_inc(out_ready, 1)

        @block.gpsimd
        def _(pool):
            def step(k, u, r):
                pool.wait_ge(y_out, k + 1)
                pool.sem_inc(pool_settled, 1)
                nc.gpsimd.indirect_dma_start(
                    y_rows, bass.IndirectOffsetOnAxis(ap=xin[u][:, D:D + 1].bitcast(U32), axis=0), y[u % SB][:, :], None
                ).then_inc(y_stored[u % SB], 16)

            tile_loop(pool, step, 0)

            def power(b):
                pool.wait_ge(ln_var, B + b + 1)
                nc.gpsimd.tensor_tensor(stats[:, b, 3, :], stats[:, b, 0, :], neg_half[:, :], ALU.pow
                                        ).then_inc(ln_pow, 1)

            for b in range(B):
                pool.wait_ge(yk_in[b], 32)
                nc.gpsimd.tensor_tensor(yk[b][:, 0], yk[b][:, 0], xall[:, tokens(b), :], ALU.add).then_inc(summed, 1)
                if b >= 2:
                    power(b - 2)
            for b in range(B - 2, B):
                power(b)

        phase.close()


def rope_tables(S):
    inv = (1.0 / 10000.0 ** (np.arange(0, DK, 2, dtype=np.float32) / np.float32(DK))).astype(np.float32)
    angles = np.outer(np.arange(S, dtype=np.float32), inv).astype(np.float32)
    lay = lambda t: np.ascontiguousarray(np.tile(np.repeat(t.astype(np.float32), 2, axis=-1).T, (H, 1)))
    return lay(np.cos(angles)), lay(np.sin(angles))


_INS = ["L0_attn_x", "L0_attn_Wq", "L0_attn_Wk", "L0_attn_Wv", "L0_attn_Wo", "L0_ffn_Wr", "L0_ffn_W1", "L0_ffn_W2"]


def kernel(**inputs):
    import concourse.bacc as bacc
    from concourse.bass_utils import run_bass_kernel_spmd as run

    nc = bacc.Bacc("TRN2", target_bir_lowering=False, num_devices=1)
    B, S, _ = inputs["L0_attn_x"].shape
    given = {n: np.ascontiguousarray(inputs[n]) for n in _INS}
    given["cos"], given["sin"] = rope_tables(S)
    arrays, args = {}, []
    for name, a in given.items():
        arrays[f"in_{name}_dram"] = a
        args.append(nc.dram_tensor(f"in_{name}_dram", a.shape, mybir.dt.from_np(a.dtype), kind="ExternalInput").ap())
    out = nc.dram_tensor("out_0_dram", (B, S, D), F32, kind="ExternalOutput").ap()
    build(nc, *args, out)
    r = run(nc, [arrays], core_ids=[0])
    return r.results[0]["out_0_dram"]
```
